# Optimizing a Trainium2 kernel written in Bass

```python
import numpy as np
import jax
import jax.numpy as jnp

def _softmax(x, axis=-1):
    return jax.nn.softmax(x, axis=axis)

def _gelu(x):
    return jax.nn.gelu(x, approximate=True)

def _silu(x):
    return jax.nn.silu(x)

def _sigmoid(x):
    return jax.nn.sigmoid(x)

def _layernorm(x, axis=-1, eps=1e-05):
    m = jnp.mean(x, axis=axis, keepdims=True)
    v = jnp.var(x, axis=axis, keepdims=True)
    return (x - m) / jnp.sqrt(v + eps)

def _scatter_add(tgt, idx, src, axis=0):
    return tgt.at[idx].add(src)

def _segment_sum(src, seg, n):
    return jax.ops.segment_sum(src, seg, n)
kernel_name = 'mk_adaln_d1_jaxref_r4_8db7de'

def setup_inputs(seed: int=0):
    np.random.seed(seed)
    _w = jnp.asarray

    def _L0_attn_setup():
        import jax, jax.numpy as jnp
        import numpy as np
        from math import sqrt
        D_MODEL = 256
        NUM_HEADS = 16
        MASK_VAL = -100000000.0

        def _proj_heads(x, w, h):
            d = w.shape[0] // h
            w = w.reshape(h, d, w.shape[1])
            return jnp.einsum('bsi,hdi->bhsd', x, w)
        key = jax.random.key(seed)
        k1, k2, k3, k4, k5 = jax.random.split(key, 5)
        scale = 1.0 / sqrt(D_MODEL)
        return {'in_features': jax.random.normal(k1, (2, 512, D_MODEL), dtype=jnp.float32), 'q_proj_weight': jax.random.normal(k2, (D_MODEL, D_MODEL), dtype=jnp.float32) * scale, 'k_proj_weight': jax.random.normal(k3, (D_MODEL, D_MODEL), dtype=jnp.float32) * scale, 'v_proj_weight': jax.random.normal(k4, (D_MODEL, D_MODEL), dtype=jnp.float32) * scale, 'o_proj_weight': jax.random.normal(k5, (D_MODEL, D_MODEL), dtype=jnp.float32) * scale}
    _L0_attn_in = _L0_attn_setup()

    def _L0_ffn_setup():
        import jax, jax.numpy as jnp
        import numpy as np
        H = 32
        MB = 2
        TOP_K = 2
        key = jax.random.key(seed)
        ks = jax.random.split(key, 8)
        B, S, D, E = (8, 256, 256, 8)
        Fd = 4 * D

        def w(k, shape, fan):
            return jax.random.normal(k, shape, jnp.float32) / np.float32(np.sqrt(fan))
        return dict(x=jax.random.normal(ks[0], (B, S, D), jnp.float32), ln_g=jnp.ones((D,), jnp.float32), ln_b=jnp.zeros((D,), jnp.float32), wq=w(ks[1], (D, D), D), wk=w(ks[2], (D, D), D), wv=w(ks[3], (D, D), D), wo=w(ks[4], (D, D), D), gate_w=w(ks[5], (E, D), D), w1=w(ks[6], (E, D, Fd), D), b1=jnp.zeros((E, Fd), jnp.float32), w2=w(ks[7], (E, Fd, D), Fd), b2=jnp.zeros((E, D), jnp.float32))
    _L0_ffn_in = _L0_ffn_setup()
    _L0_c = _w((lambda *s: np.random.randn(*s).astype(np.float32) * 0.05)(8, 256))
    _L0_wmod = _w((lambda *s: np.random.randn(*s).astype(np.float32) * 0.05)(256, 6 * 256) * 256 ** (-0.5))
    _d = {'L0_attn_in_features': _L0_attn_in['in_features'], 'L0_attn_q_proj_weight': _L0_attn_in['q_proj_weight'], 'L0_attn_k_proj_weight': _L0_attn_in['k_proj_weight'], 'L0_attn_v_proj_weight': _L0_attn_in['v_proj_weight'], 'L0_attn_o_proj_weight': _L0_attn_in['o_proj_weight'], 'L0_ffn_ln_g': _L0_ffn_in['ln_g'], 'L0_ffn_ln_b': _L0_ffn_in['ln_b'], 'L0_ffn_wq': _L0_ffn_in['wq'], 'L0_ffn_wk': _L0_ffn_in['wk'], 'L0_ffn_wv': _L0_ffn_in['wv'], 'L0_ffn_wo': _L0_ffn_in['wo'], 'L0_ffn_gate_w': _L0_ffn_in['gate_w'], 'L0_ffn_w1': _L0_ffn_in['w1'], 'L0_ffn_b1': _L0_ffn_in['b1'], 'L0_ffn_w2': _L0_ffn_in['w2'], 'L0_ffn_b2': _L0_ffn_in['b2'], 'L0_c': _L0_c, 'L0_wmod': _L0_wmod}
    _x0 = _d['L0_attn_in_features']
    _d['L0_attn_in_features'] = jax.random.normal(jax.random.fold_in(jax.random.key(seed), 1), (8, 512, 256), dtype=_x0.dtype)
    del _x0
    return _d

def reference(L0_attn_in_features, L0_attn_q_proj_weight, L0_attn_k_proj_weight, L0_attn_v_proj_weight, L0_attn_o_proj_weight, L0_ffn_ln_g, L0_ffn_ln_b, L0_ffn_wq, L0_ffn_wk, L0_ffn_wv, L0_ffn_wo, L0_ffn_gate_w, L0_ffn_w1, L0_ffn_b1, L0_ffn_w2, L0_ffn_b2, L0_c, L0_wmod):

    def _L0_attn_ref(in_features, q_proj_weight, k_proj_weight, v_proj_weight, o_proj_weight):
        import jax, jax.numpy as jnp
        import numpy as np
        from math import sqrt
        D_MODEL = 256
        NUM_HEADS = 16
        MASK_VAL = -100000000.0

        def _proj_heads(x, w, h):
            d = w.shape[0] // h
            w = w.reshape(h, d, w.shape[1])
            return jnp.einsum('bsi,hdi->bhsd', x, w)
        h = NUM_HEADS
        b, s, _ = in_features.shape
        q = _proj_heads(in_features, q_proj_weight, h)
        k = _proj_heads(in_features, k_proj_weight, h)
        v = _proj_heads(in_features, v_proj_weight, h)
        d_k = q.shape[-1]
        mask = jnp.triu(jnp.full((s, s), MASK_VAL, dtype=q.dtype), k=1)[None, None]
        scores = jnp.einsum('bhqd,bhkd->bhqk', q, k) / sqrt(d_k) + mask
        attn = jax.nn.softmax(scores, axis=-1)
        out = jnp.einsum('bhqk,bhkd->bhqd', attn, v)
        out = out.transpose(0, 2, 1, 3).reshape(b, s, -1)
        return jnp.einsum('bsv,mv->bsm', out, o_proj_weight)

    def _L0_ffn_ref(x, ln_g, ln_b, wq, wk, wv, wo, gate_w, w1, b1, w2, b2):
        import jax, jax.numpy as jnp
        import numpy as np
        H = 32
        MB = 2
        TOP_K = 2
        B, S, D = x.shape
        E = w1.shape[0]
        hd = D // H
        mu = jnp.mean(x, axis=-1, keepdims=True)
        var = jnp.var(x, axis=-1, keepdims=True)
        xn = (x - mu) / jnp.sqrt(var + 1e-05) * ln_g + ln_b
        q = (xn @ wq).reshape(B, S, H, hd)
        k = (xn @ wk).reshape(B, S, H, hd)
        v = (xn @ wv).reshape(B, S, H, hd)
        att = jnp.einsum('bqhd,bkhd->bhqk', q, k) / np.float32(np.sqrt(hd))
        p = jax.nn.softmax(att, axis=-1)
        o = jnp.einsum('bhqk,bkhd->bqhd', p, v).reshape(B, S, D) @ wo + x
        xf = o.reshape(-1, D)
        logits = xf @ gate_w.T
        _ = jax.lax.top_k(logits, TOP_K)
        tpe = xf.shape[0] // (MB * E)
        xe = xf.reshape(MB, E, tpe, D)
        h = jax.nn.gelu(jnp.einsum('metd,edf->metf', xe, w1) + b1[None, :, None, :], approximate=False)
        y = jnp.einsum('metf,efd->metd', h, w2) + b2[None, :, None, :]
        return y.reshape(B, S, D)
    x = L0_attn_in_features
    mod = (_silu(L0_c) @ L0_wmod).reshape(L0_c.shape[0], 6, 1, -1)
    sa, ca, ga, sb, cb, gb = (mod[:, 0], mod[:, 1], mod[:, 2], mod[:, 3], mod[:, 4], mod[:, 5])
    ga = (2 * (ga >= 0) - 1) * jnp.maximum(jnp.abs(ga), 0.25)
    gb = (2 * (gb >= 0) - 1) * jnp.maximum(jnp.abs(gb), 0.25)
    h = _layernorm(x, axis=-1) * (1 + ca) + sa
    x = x + ga * _L0_attn_ref(h, L0_attn_q_proj_weight, L0_attn_k_proj_weight, L0_attn_v_proj_weight, L0_attn_o_proj_weight)
    h = _layernorm(x, axis=-1) * (1 + cb) + sb
    x = x + gb * _L0_ffn_ref(h, L0_ffn_ln_g, L0_ffn_ln_b, L0_ffn_wq, L0_ffn_wk, L0_ffn_wv, L0_ffn_wo, L0_ffn_gate_w, L0_ffn_w1, L0_ffn_b1, L0_ffn_w2, L0_ffn_b2)
    return x

_drawn_inputs = setup_inputs


def setup_inputs(seed=0):
    import zlib

    import numpy as np

    out = dict(_drawn_inputs(seed))
    spreads = {'L0_ffn_ln_g': (1.0, 0.6),
     'L0_ffn_ln_b': (0.0, 0.502),
     'L0_ffn_b1': (0.0, 0.476),
     'L0_ffn_b2': (0.0, 0.322)}
    factors = {'L0_ffn_wq': 3.174, 'L0_ffn_wk': 3.109}
    for name, (base, spread) in spreads.items():
        noise = np.random.default_rng([zlib.crc32(name.encode()), seed]).standard_normal(out[name].shape)
        drawn = base * np.exp(spread * noise) if base else spread * noise
        out[name] = jnp.asarray(drawn.astype(out[name].dtype))
    for name, factor in factors.items():
        out[name] = (out[name] * factor).astype(out[name].dtype)
    return out
```

```python
from contextlib import ExitStack

import numpy as np

import concourse.bass as bass
from concourse import mybir

F32 = mybir.dt.float32
BF16 = mybir.dt.bfloat16
I32 = mybir.dt.int32
ALU = mybir.AluOpType
ACT = mybir.ActivationFunctionType
AX_X = mybir.AxisListType.X

P = 128
LN_EPS = 1e-5
GATE_MIN = 0.25
NEWTON = 3
ROOT_STEPS = 3 + 3 * NEWTON
MASKED = -1e30
LEAD = 7

HEADS = (16, 32)
WIDTH = (16, 8)
CAUSAL = (True, False)
Q_PARTS = ((0, 1, 2, 0, 1, 0), (0, 1, 2, 0, 1, 2, 0, 1, 2))
K_PARTS = ((0, 0, 0, 1, 1, 2), (0, 1, 2, 1, 2, 0, 2, 0, 1))
M_PARTS = 3
UNIT_HEADS = 16
GROUP = 4


def rows_of(a):
    return WIDTH[a] * len(Q_PARTS[a])


def runs(parts):
    out = []
    for g, part in enumerate(parts):
        if out and part == out[-1][1] + out[-1][2]:
            out[-1][2] += 1
        else:
            out.append([g, part, 1])
    return out



def attention_items(a, off):
    groups = HEADS[a] // GROUP
    last = 4 * groups
    steps = []
    for s in range(-LEAD, last + 3):
        step = []
        if 0 <= s < last:
            step.append(("scores", off, a, s))
        if s + LEAD < HEADS[a]:
            step.append(("maxima", off, a, s + LEAD))
        if (s + LEAD) % GROUP == 0 and 0 < s + LEAD <= HEADS[a]:
            step.append(("max_rows", off, a, (s + LEAD) // GROUP - 1))
        if 0 <= s - 1 < last:
            step.append(("values", off, a, s - 1))
        if s >= 6 and (s - 6) % 4 == 0:
            step.append(("normalise", off, a, (s - 6) // 4))
        steps.append(step)
    return steps


def project_items(a, off):
    return ([("v", off, a, half) for half in range(2)]
            + [("qk", off, a, t, oc) for t in range(2) for oc in range(2)])


def first_items(off):
    return ([("layernorm", off, 0)] + [("to_features", off, 0, c) for c in range(2)]
            + project_items(0, off))


def middle_items(off):
    return ([("head_features", off, 0, c) for c in range(2)]
            + [("attention_out", off, half) for half in range(2)]
            + [("layernorm", off, 1), ("ffn_input", off), ("to_features", off, 1, 0), ("to_features", off, 1, 1),
               ("layernorm", off, 2), ("to_features", off, 2, 0), ("to_features", off, 2, 1)]
            + project_items(1, off) + [("stacks", off, 1), ("stacks", off, 2)])


def both_experts(off):
    return ([("expert_in", off, 0, f) for f in range(4)] + [("load_experts", off, 1), ("expert_out", off, 0)]
            + [("expert_in", off, 1, f) for f in range(4)] + [("expert_out", off, 1)])


def flat(steps):
    return [item for step in steps for item in step]


def sections():
    def tail(off):
        return ([("head_features", off, 1, c) for c in range(2)]
                + [("ffn_sum", off, c) for c in range(2)])

    before = ([("load_x", 0)] + first_items(0) + [("stacks", 0, 0), ("load_batch", 0)] + flat(attention_items(0, 0))
              + [("load_experts", 0, 0)] + middle_items(0))
    loop = ([("load_x", 1), ("bias_part", 0)] + flat(attention_items(1, 0)) + first_items(1) + tail(0)
            + [("stacks", 1, 0)]
            + both_experts(0)
            + [("load_batch", 1), ("load_experts", 1, 0)] + flat(attention_items(0, 1)) + middle_items(1))
    after = ([("bias_part", 0)] + flat(attention_items(1, 0)) + tail(0)
             + both_experts(0))
    return (("before", before), ("loop", loop), ("after", after))


def banks_of(item):
    kind = item[0]
    if kind == "scores":
        return ["pair0", "pair1"]
    if kind == "maxima":
        return ["max0", "max1"] * 2
    if kind in ("max_rows", "normalise"):
        return ["misc"]
    if kind == "values":
        return ["out"] if item[3] % 4 == 0 else []
    if kind in ("to_features", "head_features"):
        return ["pair%d" % item[3]]
    if kind == "qk":
        return ["pair%d" % item[4]] if item[3] == 0 else ["max%d" % item[4]]
    if kind == "v":
        return ["pair%d" % item[3]]
    if kind in ("attention_out", "ffn_sum"):
        return ["max%d" % item[2]]
    if kind == "expert_in":
        return ["pair%d" % (item[3] % 2)]
    if kind == "expert_out":
        return ["max%d" % item[2]]
    return []


BANKS = ("pair0", "pair1", "max0", "max1", "out", "misc")


def number_fills(plan):
    begun = dict.fromkeys(BANKS, 0)
    fills, per_loop = {}, {}
    for name, items in plan:
        count = dict.fromkeys(BANKS, 0)
        for item in items:
            fills[name, item] = []
            for bank in banks_of(item):
                fills[name, item].append((bank, begun[bank] + count[bank]))
                count[bank] += 1
        turns = (LOOPS if name == "loop" else 1)
        if name == "loop":
            per_loop = count
        for bank in BANKS:
            begun[bank] += turns * count[bank]
    return fills, per_loop


BATCHES = 8
LOOPS = BATCHES - 1


def build(nc, x, wq1, wk1, wv1, wo1, ln_g, ln_b, wq2, wk2, wv2, wo2, w1, b1, w2, b2, c, wmod, out):
    _, S, D = x.shape
    E, _, F = w1.shape
    T = S // P
    C = D // P
    FT = F // P
    EXP_TOK = S // 2
    assert S == 512 and D == 256 and T == 4 and C == 2 and EXP_TOK == 256

    plan = sections()
    fills, per_loop = number_fills(plan)

    q_dram = [nc.dram_tensor("q_parts0", (3, D, S), BF16, kind="Internal").ap(),
              nc.dram_tensor("q_parts1", (C, 3, P, S), BF16, kind="Internal").ap()]
    k_dram = [nc.dram_tensor("k_parts0", (3, D, S), BF16, kind="Internal").ap(),
              nc.dram_tensor("k_parts1", (C, 3, P, S), BF16, kind="Internal").ap()]
    mod_dram = nc.dram_tensor("mod_rows", (BATCHES, 4 * D), F32, kind="Internal").ap()

    with ExitStack() as ctx:
        def sb(name, shape, dt=F32):
            return ctx.enter_context(nc.sbuf_tensor(name, shape, dt))

        def psum(name, shape):
            return ctx.enter_context(nc.psum_tensor(name, shape, F32))

        def sem(name):
            return ctx.enter_context(nc.semaphore(name))

        pair = [psum("pair%d" % n, [P, 2, 512]) for n in range(2)]
        maxb = [psum("max%d" % n, [P, 512]) for n in range(2)]
        outb = psum("outb", [P, 512])
        misc = psum("misc", [P, 512])
        region = {"pair0": pair[0][:, 0, :], "pair1": pair[1][:, 0, :], "max0": maxb[0][:, :], "max1": maxb[1][:, :],
                  "out": outb[:, :], "misc": misc[:, :]}

        ident = sb("ident", [P, P])
        causal = sb("causal", [P, S])
        ones_rows = sb("ones_rows", [M_PARTS, S], BF16)
        zeros = sb("zeros", [P, P], BF16)
        q_stack = [sb("q_stack%d" % n, [P, UNIT_HEADS, S], BF16) for n in range(2)]
        k_stack = [sb("k_stack%d" % n, [P, UNIT_HEADS, S], BF16) for n in range(2)]
        probs = [sb("probs%d" % n, [P, GROUP, S]) for n in range(2)]
        v_tile = [sb("v_tile%d" % a, [P, T, HEADS[a], WIDTH[a] + 1]) for a in range(2)]
        w_qkv = [[sb("w%s%d" % (n, a), [P, C, D]) for n in "qkv"] for a in range(2)]
        w_o = [sb("wo%d" % a, [P, C, D]) for a in range(2)]
        w_in = sb("w_in", [P, C, F])
        w_out = sb("w_out", [P, FT, D])
        x_in = sb("x_in", [P, T, D])
        x1 = sb("x1", [P, T, D])
        x_res = sb("x_res", [P, T, D])
        normed = [sb("normed%d" % n, [P, T, D]) for n in range(2)]
        ffn_x = normed[1]
        ffn_xT = sb("ffn_xT", [P, C, S])
        act_T = sb("act_T", [P, C, S])
        parts = [sb("parts%s" % n, [P, 3, C, S], BF16) for n in "qk"]
        rest = sb("rest", [P, 2, S])
        neg_max = sb("neg_max", [P, 2, GROUP * T])
        max_row = sb("max_row", [GROUP * T, 2, P])
        max_rest = sb("max_rest", [GROUP * T, 2, P])
        max_parts = sb("max_parts", [GROUP * T, 2, M_PARTS, P], BF16)
        out_raw = sb("out_raw", [P, 2, S])
        inv_sum = sb("inv_sum", [P, T * GROUP])
        heads = sb("heads", [P, T, D])
        heads_T = sb("heads_T", [P, C, S])
        expert_xT = sb("expert_xT", [P, C, S])
        hidden_T = sb("hidden_T", [P, FT, EXP_TOK])
        y_out = sb("y_out", [P, 2, 2, D])
        mod_bc = sb("mod_bc", [P, 3, D])
        gb_bc = sb("gb_bc", [P, D])
        b2_bc = sb("b2_bc", [P, 2, D])
        mod_T = sb("mod_T", [P, 2 * C, BATCHES])
        mod_cur = sb("mod_cur", [P, 2 * C])
        b1_T = sb("b1_T", [P, E * FT])
        b1_cur = sb("b1_cur", [P, 2, FT])
        lng_T = sb("lng_T", [P, C])
        lnb_T = sb("lnb_T", [P, C])
        stats = sb("stats", [P, 3, T, 6])
        mean_var = sb("mean_var", [P, 3, T, 2])
        rstd = sb("rstd", [P, 3, T])
        root = sb("root", [P, 3, 2, T])
        c_T = sb("c_T", [P, C, BATCHES])
        silu = sb("silu", [P, 3, C, BATCHES])
        mod_row = hidden_T[0:BATCHES, 0:4, :]
        gate_tmp = hidden_T[0:BATCHES, 4:8, :].rearrange("b (k i) d -> b k i d", k=2)
        stage_w = [t[:, :, :].rearrange("p a s -> p (a s)")[:, 0:2 * C * D].bitcast(F32).rearrange(
            "p (c d) -> p c d", c=C) for t in (q_stack[0], q_stack[1])]
        stage_w += [t[:, :, :].rearrange("p a s -> p (a s)")[:, 2 * C * D:4 * C * D].bitcast(F32).rearrange(
            "p (c d) -> p c d", c=C) for t in (q_stack[0], q_stack[1])]
        stage_w2 = [t[:, :, :].rearrange("p a s -> p (a s)")[:, 4 * C * D:6 * C * D].bitcast(F32).rearrange(
            "p (c d) -> p c d", c=C) for t in (q_stack[0], q_stack[1])]
        stage_b1 = q_stack[0][:, :, :].rearrange("p a s -> p (a s)")[:, 6 * C * D:6 * C * D + 2 * P].bitcast(F32)
        stage_mod = probs[0][:, :, :].rearrange("p a s -> p (a s)")[:, 0:C * 768].rearrange("p (c n) -> p c n", c=C)
        stage_mod2 = probs[1][:, :, :].rearrange("p a s -> p (a s)")[:, 0:C * 768].rearrange("p (c n) -> p c n", c=C)

        filled = {b: sem("filled_" + b) for b in BANKS}
        drained = {b: sem("drained_" + b) for b in BANKS}
        const_made = sem("const_made")
        small_in = sem("small_in")
        weights_in = sem("weights_in")
        mod_in = sem("mod_in")
        silu_step = sem("silu_step")
        silu_exp = sem("silu_exp")
        pro_filled = sem("pro_filled")
        pro_drained = sem("pro_drained")
        gate_step = sem("gate_step")
        mod_rows_made = sem("mod_rows_made")
        mod_stored = sem("mod_stored")
        stage_done = sem("stage_done")
        perm_done = sem("perm_done")
        ones_made = sem("ones_made")
        waits_passed = sem("waits_passed")
        x_loaded = sem("x_loaded")
        mod_loaded = sem("mod_loaded")
        gate_loaded = sem("gate_loaded")
        mod_cur_made = sem("mod_cur_made")
        stats_made = [sem("stats_made%d" % n) for n in range(3)]
        moments_made = [sem("moments_made%d" % n) for n in range(3)]
        rstd_made = [sem("rstd_made%d" % n) for n in range(3)]
        normed_made = [sem("normed_made%d" % n) for n in range(3)]
        features_made = [sem("features_made%d" % n) for n in range(3)]
        top_made = [sem("top_made%d" % a) for a in range(2)]
        second_made = [sem("second_made%d" % a) for a in range(2)]
        split_made = [sem("split_made%d" % a) for a in range(2)]
        parts_stored = [sem("parts_stored%d" % a) for a in range(2)]
        stack_loaded = [sem("stack_loaded%d" % u) for u in range(3)]
        max_split = [sem("max_split%d" % a) for a in range(2)]
        max_stored = [[sem("max_stored%d%d" % (a, n)) for n in range(2)] for a in range(2)]
        masked_made = sem("masked_made")
        values_done = [sem("values_done%d" % a) for a in range(2)]
        sums_inverted = [sem("sums_inverted%d" % a) for a in range(2)]
        x1_gated = sem("x1_gated")
        x1_made = sem("x1_made")
        ffn_scaled = sem("ffn_scaled")
        ffn_x_made = sem("ffn_x_made")
        bias_gated = sem("bias_gated")
        res_made = sem("res_made")
        w_in_loaded = sem("w_in_loaded")
        w_out_loaded = sem("w_out_loaded")
        b1_made = sem("b1_made")
        y_made = sem("y_made")
        y_stored = [sem("y_stored%d" % j) for j in range(2)]

        w_view = [(w, i) for i, w in enumerate((wq1, wk1, wv1, wo1))]

        def number(fill, turn):
            bank, n = fill
            return n if turn is None else turn * per_loop[bank] + n

        def wait(eng, semaphore, value):
            if isinstance(value, int) and value <= 0:
                return
            eng.wait_ge(semaphore, value)

        def wait_apart(eng, semaphore, value):
            wait(eng, semaphore, value)
            if not isinstance(value, int):
                eng.sem_inc(waits_passed, 1)

        def walk(eng, share):
            for name, items in plan:
                if name == "loop":
                    with eng.Fori(0, LOOPS) as turn:
                        for item in items:
                            if item[0] in share:
                                share[item[0]](turn + item[1] if item[1] else turn, turn, fills[name, item], *item[2:])
                else:
                    b = 0 if name == "before" else BATCHES - 1
                    for item in items:
                        if item[0] in share:
                            share[item[0]](b, None, fills[name, item], *item[2:])

        unit_of = lambda a, h: 0 if a == 0 else 1 + h // UNIT_HEADS
        side_of = lambda u: u % 2
        STACK_DMAS = [len(runs(Q_PARTS[a])) + len(runs(K_PARTS[a])) for a in range(2)]
        stack_dmas = [STACK_DMAS[0], STACK_DMAS[1], STACK_DMAS[1] + 1]

        steps_of = [T * h // GROUP for h in HEADS]

        block = ctx.enter_context(nc.Block())

        @block.sync
        def _(sp):
            for j in range(2):
                sp.sem_inc(y_stored[j], 1)
            with nc.allow_non_contiguous_dma("a few kilobytes"):
                for cc in range(C):
                    sp.dma_start(c_T[:, cc, :], c[:, cc * P:(cc + 1) * P].rearrange("b p -> p b")).then_inc(small_in, 16)
                sp.dma_start(lng_T[:, :], ln_g.rearrange("(c p) -> p c", p=P)).then_inc(small_in, 16)
                sp.dma_start(lnb_T[:, :], ln_b.rearrange("(c p) -> p c", p=P)).then_inc(small_in, 16)
            sp.dma_start(stage_mod, wmod[:, 0:768].rearrange("(c p) n -> p c n", p=P)).then_inc(mod_in, 16)
            sp.dma_start(stage_mod2, wmod[:, 768:1536].rearrange("(c p) n -> p c n", p=P)).then_inc(mod_in, 16)
            sp.dma_start(stage_b1[0:E * FT, :], b1.rearrange("e (f p) -> (e f) p", p=P)).then_inc(weights_in, 16)
            for w, i in w_view:
                sp.dma_start(stage_w[i], w.rearrange("(c p) n -> p c n", p=P)).then_inc(weights_in, 16)
            for w, st in ((wq2, stage_w2[0]), (wk2, stage_w2[1]), (wv2, w_qkv[1][2][:, :, :]), (wo2, w_o[1][:, :, :])):
                sp.dma_start(st, w.rearrange("(c p) n -> p c n", p=P)).then_inc(weights_in, 16)
            sp.wait_ge(mod_rows_made, 6)
            sp.dma_start(mod_dram[:, :], mod_row[:, :, :].rearrange("b v d -> b (v d)")).then_inc(mod_stored, 16)
            sp.wait_ge(mod_stored, 16)

            def load_x(b, turn, f):
                wait_apart(sp, x1_made, 2 * b)
                sp.dma_start(x_in[:, :, :], x[b].rearrange("(t p) d -> p t d", p=P)).then_inc(x_loaded, 16)

            def load_batch(b, turn, f):
                wait_apart(sp, ffn_x_made, T * b)
                sp.dma_start(mod_bc[:, :, :].rearrange("p v d -> p (v d)"),
                             mod_dram[b, 0:3 * D].partition_broadcast(P)).then_inc(mod_loaded, 16)
                wait_apart(sp, y_made, 2 * b)
                sp.dma_start(gb_bc[:, :], mod_dram[b, 3 * D:4 * D].partition_broadcast(P)).then_inc(gate_loaded, 16)
                for j in range(2):
                    sp.dma_start(b2_bc[:, j, :], b2[(b * 2 + j) % E].partition_broadcast(P)).then_inc(gate_loaded, 16)

            hidden_fill = {}

            def expert_in(b, turn, f, j, n):
                hidden_fill[0] = f[0]

            def load_experts(b, turn, f, j):
                e = (b * 2 + j) % E
                if j == 0:
                    wait_apart(sp, y_made, 2 * b)
                else:
                    bank, _ = hidden_fill[0]
                    wait_apart(sp, filled[bank], number(hidden_fill[0], turn) + 1)
                sp.dma_start(w_in[:, :, :], w1[e].rearrange("(c p) n -> p c n", p=P)).then_inc(w_in_loaded, 16)
                if j == 1:
                    wait_apart(sp, y_made, 2 * b + 1)
                sp.dma_start(w_out[:, :, :], w2[e].rearrange("(f p) n -> p f n", p=P)).then_inc(w_out_loaded, 16)

            def qk(b, turn, f, a, t, oc):
                n = 2 * t + oc
                if n == 0:
                    for u in ((0,), (1, 2))[a]:
                        wait_apart(sp, stack_loaded[u], 16 * stack_dmas[u] * b)
                wait_apart(sp, split_made[a], 4 * b + n + 1)
                dram = (q_dram, k_dram)[t][a]
                if a == 0:
                    dst = dram[:, oc * P:(oc + 1) * P, :]
                else:
                    dst = dram[oc]
                sp.dma_start(dst.rearrange("i p s -> p i s"), parts[t][:, :, oc, :]).then_inc(parts_stored[a], 16)

            def stacks(b, turn, f, u):
                a = min(u, 1)
                d = WIDTH[a]
                side = side_of(u)
                wait_apart(sp, parts_stored[a], 16 * 4 * (b + 1))
                if u == 0:
                    wait_apart(sp, values_done[1], steps_of[1] * b)
                elif u == 1:
                    wait_apart(sp, values_done[1], steps_of[1] * (b - 1) + steps_of[1] // 2)
                else:
                    wait_apart(sp, values_done[0], steps_of[0] * (b + 1))
                for dram, stack, order in ((q_dram, q_stack, Q_PARTS[a]), (k_dram, k_stack, K_PARTS[a])):
                    if a == 0:
                        src = dram[0].rearrange("i (d h) s -> (i d) (h s)", d=d)
                    else:
                        src = dram[1][u - 1].rearrange("i (d h) s -> (i d) (h s)", d=d)
                    dst = stack[side][:, :, :].rearrange("p h s -> p (h s)")
                    for g, part, n in runs(order):
                        sp.dma_start(dst[g * d:(g + n) * d, :], src[part * d:(part + n) * d, :])\
                          .then_inc(stack_loaded[u], 16)
                if u == 2:
                    r = rows_of(1)
                    sp.dma_start(k_stack[side][r:r + M_PARTS, :, :],
                                 ones_rows[:, :].unsqueeze(1).broadcast_to([M_PARTS, UNIT_HEADS, S]))\
                      .then_inc(stack_loaded[u], 16)

            def max_rows(b, turn, f, a, g):
                groups = HEADS[a] // GROUP
                u = unit_of(a, g * GROUP)
                r, h = rows_of(a), g * GROUP % UNIT_HEADS
                wait_apart(sp, max_split[a], 4 * groups * b + 4 * g + 4)
                for m in range(M_PARTS):
                    dst = q_stack[side_of(u)][r + m:r + m + 1, h:h + GROUP, :].rearrange("p h (q t) -> p (h q) t", t=P)
                    sp.dma_start(dst, max_parts[:, g % 2, m, :]).then_inc(max_stored[a][g % 2], 16)

            def expert_out(b, turn, f, j):
                wait_apart(sp, y_made, 2 * b + j + 1)
                half = out[b].rearrange("(j t p) d -> j p t d", j=2, p=P)[j]
                sp.dma_start(half, y_out[:, j, :, :]).then_inc(y_stored[j], 16)

            walk(sp, {"load_x": load_x, "load_batch": load_batch, "load_experts": load_experts, "qk": qk,
                      "stacks": stacks, "max_rows": max_rows, "expert_in": expert_in, "expert_out": expert_out})
            for j in range(2):
                sp.wait_ge(y_stored[j], 16 * BATCHES + 1)

        @block.gpsimd
        def _(pool):
            pool.memset(ident[:, :], 0.0).then_inc(const_made, 1)
            pool.memset(causal[:, :], 0.0).then_inc(const_made, 1)
            pool.memset(zeros[:, :], 0.0).then_inc(const_made, 1)
            pool.memset(ones_rows[:, :], 1.0).then_inc(const_made, 1)
            for a in range(2):
                pool.memset(v_tile[a][:, :, :, WIDTH[a]:WIDTH[a] + 1], 1.0).then_inc(const_made, 1)
            pool.wait_ge(const_made, 6)
            pool.affine_select(out=ident[:, :], in_=ident[:, :], compare_op=ALU.not_equal, fill=1.0, base=0,
                               pattern=[[-1, P]], channel_multiplier=1).then_inc(const_made, 1)
            pool.affine_select(out=causal[:, S - P:S], in_=causal[:, S - P:S], compare_op=ALU.is_ge, fill=MASKED,
                               base=0, pattern=[[-1, P]], channel_multiplier=1).then_inc(const_made, 1)
            for n in range(2):
                pool.memset(k_stack[n][:, :, :], 1.0).then_inc(ones_made, 1)

            def qk(b, turn, f, a, t, oc):
                n = 4 * b + 2 * t + oc
                buf = (2 * t + oc) % 2
                bank, _ = f[0]
                wait_apart(pool, drained[bank], number(f[0], turn) + 1)
                if t == 0 and oc == 0:
                    if a == 0:
                        wait_apart(pool, parts_stored[1], 64 * b)
                    else:
                        wait_apart(pool, parts_stored[0], 64 * (b + 1))
                pool.tensor_copy(parts[t][:, 1, oc, :], rest[:, buf, :]).then_inc(second_made[a], 1)
                wait(pool, second_made[a], n + 1)
                pool.tensor_tensor(parts[t][:, 2, oc, :], rest[:, buf, :], parts[t][:, 1, oc, :], ALU.subtract)\
                    .then_inc(split_made[a], 1)

            def max_rows(b, turn, f, a, g):
                groups = HEADS[a] // GROUP
                n = 4 * groups * b + 4 * g
                buf = g % 2
                wait(pool, drained["misc"], number(f[0], turn) + 1)
                per = 48 * (groups // 2)
                if g >= 2:
                    wait_apart(pool, max_stored[a][buf], per * b + 48 * (g // 2))
                elif a == 1:
                    wait_apart(pool, max_stored[0][buf], 48 * (HEADS[0] // GROUP // 2) * (b + 1))
                else:
                    wait_apart(pool, max_stored[1][buf], 48 * (HEADS[1] // GROUP // 2) * b)
                pool.tensor_copy(max_parts[:, buf, 0, :], max_row[:, buf, :]).then_inc(max_split[a], 1)
                wait(pool, max_split[a], n + 1)
                pool.tensor_tensor(max_rest[:, buf, :], max_row[:, buf, :], max_parts[:, buf, 0, :], ALU.subtract)\
                    .then_inc(max_split[a], 1)
                wait_apart(pool, max_split[a], n + 2)
                pool.tensor_copy(max_parts[:, buf, 1, :], max_rest[:, buf, :]).then_inc(max_split[a], 1)
                wait(pool, max_split[a], n + 3)
                pool.tensor_tensor(max_parts[:, buf, 2, :], max_rest[:, buf, :], max_parts[:, buf, 1, :],
                                   ALU.subtract).then_inc(max_split[a], 1)

            def scores(b, turn, f, a, s):
                if not CAUSAL[a]:
                    return
                for bank, n in f:
                    wait_apart(pool, drained[bank], number((bank, n), turn) + 1)
                q0 = (s % T) * P
                tile = probs[s % 2][:, :, q0:q0 + P]
                pool.affine_select(out=tile, in_=tile, compare_op=ALU.is_ge, fill=0.0, base=0,
                                   pattern=[[0, GROUP], [1, P]], channel_multiplier=-1).then_inc(masked_made, 1)

            walk(pool, {"qk": qk, "max_rows": max_rows, "scores": scores})

        @block.scalar
        def _(act):
            act.wait_ge(small_in, 64)
            nc.scalar.activation(silu[:, 0, :, :], c_T[:, :, :], ACT.Exp, scale=-1.0).then_inc(silu_exp, 1)

            def qk(b, turn, f, a, t, oc):
                (bank, n), = f
                wait(act, filled[bank], number(f[0], turn) + 1)
                if t == 0 and oc == 0:
                    if a == 0:
                        wait(act, parts_stored[1], 64 * b)
                    else:
                        wait(act, parts_stored[0], 64 * (b + 1))
                nc.scalar.activation(parts[t][:, 0, oc, :], region[bank], ACT.Copy).then_inc(top_made[a], 1)

            def v(b, turn, f, a, half):
                (bank, n), = f
                wait(act, filled[bank], number(f[0], turn) + 1)
                d = WIDTH[a]
                nc.scalar.activation(v_tile[a][:, 2 * half:2 * half + 2, :, 0:d],
                                     region[bank].rearrange("p (t h d) -> p t h d", t=2, d=d), ACT.Copy)\
                    .then_inc(drained[bank], 1)

            def to_features(b, turn, f, n, cc):
                if n == 0:
                    return
                (bank, _), = f
                wait(act, filled[bank], number(f[0], turn) + 1)
                if n == 1:
                    nc.scalar.activation(ffn_xT[:, cc, :], region[bank], ACT.Copy).then_inc(drained[bank], 1)
                else:
                    nc.scalar.activation(act_T[:, cc, :], region[bank], ACT.Identity, bias=lnb_T[:, cc:cc + 1],
                                         scale=lng_T[:, cc:cc + 1]).then_inc(drained[bank], 1)

            def scores(b, turn, f, a, s):
                q0 = (s % T) * P if CAUSAL[a] else 0
                steps = [T * h // GROUP for h in HEADS]
                if s >= 2:
                    wait(act, values_done[a], steps[a] * b + s - 1)
                elif a == 1:
                    wait(act, values_done[0], steps[0] * (b + 1))
                else:
                    wait(act, values_done[1], steps[1] * b)
                for n, (bank, _) in enumerate(f):
                    wait(act, filled[bank], number(f[n], turn) + 1)
                    nc.scalar.activation(probs[s % 2][:, 2 * n:2 * n + 2, q0:S], pair[n][:, :, q0:S], ACT.Exp,
                                         scale=float(WIDTH[a]) ** -0.5).then_inc(drained[bank], 1)

            def values(b, turn, f, a, s):
                if s % T != T - 1:
                    return
                g = s // T
                steps = T * HEADS[a] // GROUP
                wait(act, values_done[a], steps * b + s + 1)
                groups = HEADS[a] // GROUP
                if g >= 2:
                    wait(act, sums_inverted[a], groups * b + g - 1)
                elif a == 1:
                    wait(act, sums_inverted[0], HEADS[0] // GROUP * (b + 1))
                else:
                    wait(act, sums_inverted[1], HEADS[1] // GROUP * b)
                nc.scalar.activation(out_raw[:, g % 2, :], outb[:, :], ACT.Copy).then_inc(drained["out"], 1)

            def head_features(b, turn, f, a, cc):
                (bank, _), = f
                wait(act, filled[bank], number(f[0], turn) + 1)
                nc.scalar.activation(heads_T[:, cc, :], region[bank], ACT.Copy).then_inc(drained[bank], 1)

            def expert_in(b, turn, f, j, n):
                (bank, _), = f
                wait(act, filled[bank], number(f[0], turn) + 1)
                if n == 0:
                    wait(act, b1_made, 2 * (b + 1))
                    if j == 1:
                        wait(act, y_made, 2 * b + 1)
                for k in range(2):
                    ins = nc.scalar.activation(hidden_T[:, 2 * n + k, :], region[bank][:, k * 256:(k + 1) * 256],
                                               ACT.Gelu, bias=b1_cur[:, j, 2 * n + k:2 * n + k + 1])
                ins.then_inc(drained[bank], 1)

            walk(act, {"qk": qk, "v": v, "to_features": to_features, "scores": scores, "values": values,
                       "head_features": head_features, "expert_in": expert_in})

        @block.tensor
        def _(pe):
            pe.wait_ge(const_made, 8)
            for k in range(4):
                pe.matmul(outb[:, k * P:(k + 1) * P], zeros[:, :], zeros[:, :], start=True, stop=True)
            pe.wait_ge(weights_in, 16 * 9)
            n = 0
            for i in range(4):
                for ic in range(C):
                    if n >= 2:
                        pe.wait_ge(pro_drained, n - 1)
                    for oc in range(C):
                        ins = pe.transpose(maxb[n % 2][:, oc * P:(oc + 1) * P], stage_w[i][:, oc, ic * P:(ic + 1) * P],
                                           ident[:, :])
                    ins.then_inc(pro_filled, 1)
                    n += 1
            pe.wait_ge(pro_drained, n - 1)
            pe.transpose(maxb[0][:, 0:E * FT], stage_b1[0:E * FT, :], ident[0:E * FT, 0:E * FT]).then_inc(pro_filled, 1)
            pe.wait_ge(mod_in, 32)
            pe.wait_ge(silu_step, 3)
            stages = (stage_mod, stage_mod2)
            for bank, lo, hi in ((pair[0][:, 0, :], 512, 768), (pair[0][:, 1, :], 768, 1280), (pair[1][:, 0, :], 1280, 1536)):
                st, o = (stages[0], 0) if hi <= 768 else (stages[1], 768)
                for cc in range(C):
                    ins = pe.matmul(bank[0:BATCHES, 0:hi - lo], silu[:, 0, cc, :], st[:, cc, lo - o:hi - o],
                                    start=(cc == 0), stop=(cc == C - 1))
                ins.then_inc(pro_filled, 1)
            for k in range(2 * C):
                for cc in range(C):
                    ins = pe.matmul(pair[1][:, 1, k * BATCHES:(k + 1) * BATCHES], stages[0][:, cc, k * P:(k + 1) * P],
                                    silu[:, 0, cc, :], start=(cc == 0), stop=(cc == C - 1))
            ins.then_inc(pro_filled, 1)
            pe.wait_ge(pro_drained, 9)
            pe.wait_ge(mod_rows_made, 6)
            pe.wait_ge(perm_done, 4)

            def start_fill(f, turn):
                bank, _ = f
                wait(pe, drained[bank], number(f, turn))

            def to_features(b, turn, f, n, cc):
                (bank, _), = f
                start_fill(f[0], turn)
                if n == 1:
                    wait(pe, ffn_x_made, T * (b + 1))
                    src = ffn_x
                else:
                    wait(pe, normed_made[n], T * (b + 1))
                    src = normed[n % 2]
                for t in range(T):
                    ins = pe.transpose(region[bank][:, t * P:(t + 1) * P], src[:, t, cc * P:(cc + 1) * P], ident[:, :])
                ins.then_inc(filled[bank], 1)

            last_features = {}

            def to_features_noted(b, turn, f, n, cc):
                to_features(b, turn, f, n, cc)
                last_features[n, cc] = f[0]

            def features_ready(turn, a):
                for cc in range(C):
                    bank, _ = last_features[2 * a, cc]
                    wait(pe, drained[bank], number(last_features[2 * a, cc], turn) + 1)

            def qk(b, turn, f, a, t, oc):
                (bank, _), = f
                start_fill(f[0], turn)
                for cc in range(C):
                    ins = pe.matmul(region[bank], w_qkv[a][t][:, cc, oc * P:(oc + 1) * P], act_T[:, cc, :],
                                    start=(cc == 0), stop=(cc == C - 1))
                ins.then_inc(filled[bank], 1)

            def v(b, turn, f, a, half):
                (bank, _), = f
                if half == 0:
                    features_ready(turn, a)
                start_fill(f[0], turn)
                for k in range(2):
                    t = 2 * half + k
                    for cc in range(C):
                        ins = pe.matmul(region[bank][:, k * D:(k + 1) * D], act_T[:, cc, t * P:(t + 1) * P],
                                        w_qkv[a][2][:, cc, :], start=(cc == 0), stop=(cc == C - 1))
                ins.then_inc(filled[bank], 1)

            last_maxima = {}

            def maxima(b, turn, f, a, h):
                u = unit_of(a, h)
                if h % UNIT_HEADS == 0:
                    wait(pe, stack_loaded[u], 16 * stack_dmas[u] * (b + 1))
                side, hh, r = side_of(u), h % UNIT_HEADS, rows_of(a)
                for qt in range(T):
                    bank, _ = f[qt]
                    keys = (qt + 1) * P if CAUSAL[a] else S
                    start_fill(f[qt], turn)
                    pe.matmul(region[bank][:, 0:keys], q_stack[side][0:r, hh, qt * P:(qt + 1) * P],
                              k_stack[side][0:r, hh, 0:keys], start=True, stop=True).then_inc(filled[bank], 1)
                last_maxima[0] = f[2:]

            def max_rows(b, turn, f, a, g):
                for bank, n in last_maxima[0]:
                    wait(pe, drained[bank], number((bank, n), turn) + 1)
                start_fill(f[0], turn)
                pe.transpose(misc[0:GROUP * T, 0:P], neg_max[:, g % 2, :], ident[:, :]).then_inc(filled["misc"], 1)

            def scores(b, turn, f, a, s):
                g, kt = s // T, s % T
                u = unit_of(a, g * GROUP)
                side, r = side_of(u), rows_of(a) + M_PARTS
                q0 = kt * P if CAUSAL[a] else 0
                if kt == 0:
                    groups = HEADS[a] // GROUP
                    wait(pe, max_stored[a][g % 2], 48 * (groups // 2) * b + 48 * (g // 2 + 1))
                for n, (bank, _) in enumerate(f):
                    start_fill(f[n], turn)
                    for k in range(2):
                        h = (g * GROUP + 2 * n + k) % UNIT_HEADS
                        ins = pe.matmul(pair[n][:, k, q0:S], k_stack[side][0:r, h, kt * P:(kt + 1) * P],
                                        q_stack[side][0:r, h, q0:S], start=True, stop=True)
                    ins.then_inc(filled[bank], 1)
                last_scores[s % 2] = f

            last_scores = {}

            def values(b, turn, f, a, s):
                g, kt = s // T, s % T
                q0 = kt * P if CAUSAL[a] else 0
                if kt == 0:
                    start_fill(f[0], turn)
                for fill in last_scores[s % 2]:
                    wait(pe, drained[fill[0]], number(fill, turn) + 1)
                if CAUSAL[a]:
                    wait(pe, masked_made, T * HEADS[a] // GROUP * b + s + 1)
                for k in range(GROUP):
                    ins = pe.matmul(outb[32 * k:32 * k + WIDTH[a] + 1, q0:S], v_tile[a][:, kt, g * GROUP + k, :],
                                    probs[s % 2][:, k, q0:S], start=(kt == 0), stop=(kt == T - 1),
                                    skip_group_check=True)
                ins.then_inc(values_done[a], 1)

            def normalise(b, turn, f, a, g):
                wait(pe, drained["out"], out_number(b, a, g) + 1)
                start_fill(f[0], turn)
                for t in range(T):
                    ins = pe.transpose(misc[:, t * P:(t + 1) * P], out_raw[:, g % 2, t * P:(t + 1) * P], ident[:, :])
                ins.then_inc(filled["misc"], 1)

            def out_number(b, a, g):
                per = (HEADS[0] + HEADS[1]) // GROUP
                return b * per + (HEADS[0] // GROUP if a else 0) + g

            def head_features(b, turn, f, a, cc):
                (bank, _), = f
                start_fill(f[0], turn)
                if cc == 0:
                    wait(pe, drained["misc"], number(last_misc[0], turn) + 1)
                for t in range(T):
                    ins = pe.transpose(region[bank][:, t * P:(t + 1) * P], heads[:, t, cc * P:(cc + 1) * P], ident[:, :])
                ins.then_inc(filled[bank], 1)
                last_heads[cc] = f[0]

            last_heads = {}
            last_misc = {}

            def normalise_noted(b, turn, f, a, g):
                normalise(b, turn, f, a, g)
                last_misc[0] = f[0]

            def heads_ready(turn):
                for cc in range(C):
                    bank, _ = last_heads[cc]
                    wait(pe, drained[bank], number(last_heads[cc], turn) + 1)

            def attention_out(b, turn, f, half):
                (bank, _), = f
                heads_ready(turn)
                start_fill(f[0], turn)
                for k in range(2):
                    t = 2 * half + k
                    for cc in range(C):
                        ins = pe.matmul(region[bank][:, k * D:(k + 1) * D], heads_T[:, cc, t * P:(t + 1) * P],
                                        w_o[0][:, cc, :], start=(cc == 0), stop=(cc == C - 1))
                ins.then_inc(filled[bank], 1)

            def ffn_sum(b, turn, f, mc):
                (bank, _), = f
                heads_ready(turn)
                start_fill(f[0], turn)
                for cc in range(C):
                    ins = pe.matmul(region[bank], w_o[1][:, cc, mc * P:(mc + 1) * P], heads_T[:, cc, :],
                                    start=(cc == 0), stop=(cc == C - 1))
                ins.then_inc(filled[bank], 1)
                last_sum[mc] = f[0]

            last_sum = {}
            last_hidden = {}

            def expert_in(b, turn, f, j, n):
                (bank, _), = f
                if n == 0:
                    wait(pe, w_in_loaded, 16 * (2 * b + j + 1))
                    if j == 0:
                        for mc in range(C):
                            wait(pe, drained[last_sum[mc][0]], number(last_sum[mc], turn) + 1)
                start_fill(f[0], turn)
                for k in range(2):
                    ft = 2 * n + k
                    for cc in range(C):
                        ins = pe.matmul(region[bank][:, k * EXP_TOK:(k + 1) * EXP_TOK],
                                        w_in[:, cc, ft * P:(ft + 1) * P],
                                        expert_xT[:, cc, j * EXP_TOK:(j + 1) * EXP_TOK],
                                        start=(cc == 0), stop=(cc == C - 1))
                ins.then_inc(filled[bank], 1)
                last_hidden[n] = f[0]

            def expert_out(b, turn, f, j):
                (bank, _), = f
                start_fill(f[0], turn)
                wait(pe, w_out_loaded, 16 * (2 * b + j + 1))
                for n in range(4):
                    wait(pe, drained[last_hidden[n][0]], number(last_hidden[n], turn) + 1)
                for k in range(2):
                    for ft in range(FT):
                        ins = pe.matmul(region[bank][:, k * D:(k + 1) * D], hidden_T[:, ft, k * P:(k + 1) * P],
                                        w_out[:, ft, :], start=(ft == 0), stop=(ft == FT - 1))
                ins.then_inc(filled[bank], 1)

            walk(pe, {"to_features": to_features_noted, "qk": qk, "v": v, "maxima": maxima,
                      "max_rows": max_rows, "scores": scores, "values": values, "normalise": normalise_noted,
                      "head_features": head_features, "attention_out": attention_out, "ffn_sum": ffn_sum,
                      "expert_in": expert_in, "expert_out": expert_out})

        @block.vector
        def _(dve):
            v = nc.vector
            dve.wait_ge(silu_exp, 1)
            v.tensor_scalar(silu[:, 1, :, :], silu[:, 0, :, :], 1.0, None, ALU.add).then_inc(silu_step, 1)
            dve.wait_ge(silu_step, 1)
            v.reciprocal(silu[:, 2, :, :], silu[:, 1, :, :]).then_inc(silu_step, 1)
            dve.wait_ge(silu_step, 2)
            v.tensor_tensor(silu[:, 0, :, :], silu[:, 2, :, :], c_T[:, :, :], ALU.mult).then_inc(silu_step, 1)
            n = 0
            for i in range(4):
                for ic in range(C):
                    dve.wait_ge(pro_filled, n + 1)
                    src = maxb[n % 2][:, 0:D]
                    if i < 2:
                        d = WIDTH[0]
                        v.tensor_copy(w_qkv[0][i][:, ic, :].rearrange("p (d h) -> p h d", d=d),
                                      src.rearrange("p (h d) -> p h d", d=d)).then_inc(pro_drained, 1)
                    else:
                        dst = w_qkv[0][2] if i == 2 else w_o[0]
                        v.tensor_copy(dst[:, ic, :], src).then_inc(pro_drained, 1)
                    n += 1
            dve.wait_ge(pro_filled, n + 1)
            v.tensor_copy(b1_T[:, :], maxb[0][:, 0:E * FT]).then_inc(pro_drained, 1)
            d = WIDTH[1]
            for t in range(2):
                for ic in range(C):
                    v.tensor_copy(w_qkv[1][t][:, ic, :].rearrange("p (c d h) -> p c h d", c=C, d=d),
                                  stage_w2[t][:, ic, :].rearrange("p (c h d) -> p c h d", c=C, d=d)).then_inc(perm_done, 1)
            dve.wait_ge(pro_filled, n + 4)
            for k, src in ((0, pair[0][0:BATCHES, 0, 0:D]), (1, pair[1][0:BATCHES, 0, 0:D])):
                v.tensor_scalar(gate_tmp[:, k, 0, :], src, 0.0, 2.0, ALU.is_ge, ALU.mult).then_inc(gate_step, 1)
                v.tensor_scalar(gate_tmp[:, k, 1, :], src, -1.0, None, ALU.mult).then_inc(gate_step, 1)
            dve.wait_ge(gate_step, 4)
            for k, src in ((0, pair[0][0:BATCHES, 0, 0:D]), (1, pair[1][0:BATCHES, 0, 0:D])):
                v.tensor_tensor(gate_tmp[:, k, 1, :], src, gate_tmp[:, k, 1, :], ALU.max).then_inc(gate_step, 1)
            dve.wait_ge(gate_step, 6)
            v.tensor_scalar(gate_tmp[:, :, 1, :], gate_tmp[:, :, 1, :], GATE_MIN, None, ALU.max).then_inc(gate_step, 1)
            dve.wait_ge(gate_step, 7)
            for k, row in ((0, 0), (1, 3)):
                v.scalar_tensor_tensor(out=mod_row[:, row, :], in0=gate_tmp[:, k, 0, :], scalar=-1.0,
                                       in1=gate_tmp[:, k, 1, :], op0=ALU.add, op1=ALU.mult).then_inc(mod_rows_made, 1)
            v.tensor_scalar(mod_row[:, 1, :], pair[0][0:BATCHES, 1, D:2 * D], 1.0, None, ALU.add).then_inc(mod_rows_made, 1)
            v.tensor_copy(mod_row[:, 2, :], pair[0][0:BATCHES, 1, 0:D]).then_inc(mod_rows_made, 1)
            dve.wait_ge(pro_filled, n + 5)
            cols = pair[1][:, 1, 0:2 * C * BATCHES].rearrange("p (k b) -> p k b", b=BATCHES)
            v.tensor_copy(mod_T[:, 0:C, :], cols[:, 0:C, :]).then_inc(mod_rows_made, 1)
            v.tensor_scalar(mod_T[:, C:2 * C, :], cols[:, C:2 * C, :], 1.0, None, ALU.add).then_inc(mod_rows_made, 1)
            dve.wait_ge(mod_rows_made, 6)
            dve.wait_ge(const_made, 8)

            def inverse_root(b, n):
                a, y, t = root[:, n, 0, :], rstd[:, n, :], root[:, n, 1, :]
                step = iter(range(ROOT_STEPS))

                def then(ins):
                    done = ROOT_STEPS * b + next(step) + 1
                    ins.then_inc(rstd_made[n], 1)
                    wait(dve, rstd_made[n], done)

                then(v.tensor_scalar(a, mean_var[:, n, :, 1], LN_EPS, None, ALU.add))
                then(v.tensor_scalar(t.bitcast(I32), a.bitcast(I32), 1, None, ALU.logical_shift_right))
                then(v.tensor_scalar(y.bitcast(I32), t.bitcast(I32), -1.0, float(0x5F3759DF), ALU.mult, ALU.add))
                for _ in range(NEWTON):
                    then(v.scalar_tensor_tensor(out=t, in0=y, scalar=-0.5, in1=y, op0=ALU.mult, op1=ALU.mult))
                    then(v.tensor_tensor(t, t, a, ALU.mult))
                    then(v.scalar_tensor_tensor(out=y, in0=t, scalar=1.5, in1=y, op0=ALU.add, op1=ALU.mult))

            def layernorm(b, turn, f, n):
                src = (x_in, x1, ffn_x)[n]
                dst = normed[n % 2]
                if n == 0:
                    wait(dve, x_loaded, 16 * (b + 1))
                    v.tensor_copy(mod_cur[:, :], mod_T[:, :, bass.ds(b, 1)].rearrange("p k b -> p (k b)"))\
                        .then_inc(mod_cur_made, 1)
                elif n == 1:
                    wait(dve, x1_made, 2 * (b + 1))
                else:
                    wait(dve, ffn_x_made, T * (b + 1))
                for t in range(T):
                    v.bn_stats(stats[:, n, t, :], src[:, t, :]).then_inc(stats_made[n], 1)
                for t in range(T):
                    wait_apart(dve, stats_made[n], T * b + t + 1)
                    v.bn_aggr(mean_var[:, n, t, :], stats[:, n, t, :]).then_inc(moments_made[n], 1)
                wait(dve, moments_made[n], T * (b + 1))
                inverse_root(b, n)
                for t in range(T):
                    v.tensor_scalar(dst[:, t, :], src[:, t, :], mean_var[:, n, t, 0:1], rstd[:, n, t:t + 1],
                                    ALU.subtract, ALU.mult).then_inc(normed_made[n], 1)

            def to_features(b, turn, f, n, cc):
                if n:
                    return
                (bank, _), = f
                wait(dve, filled[bank], number(f[0], turn) + 1)
                if cc == 0:
                    wait(dve, mod_cur_made, b + 1)
                v.tensor_scalar(act_T[:, cc, :], region[bank], mod_cur[:, C + cc:C + cc + 1], mod_cur[:, cc:cc + 1],
                                ALU.mult, ALU.add).then_inc(drained[bank], 1)

            def qk(b, turn, f, a, t, oc):
                (bank, _), = f
                n = 2 * t + oc
                wait(dve, top_made[a], 4 * b + n + 1)
                if n >= 2:
                    wait(dve, split_made[a], 4 * b + n - 1)
                elif a == 0:
                    wait(dve, split_made[1], 4 * b)
                else:
                    wait(dve, split_made[0], 4 * (b + 1))
                v.tensor_tensor(rest[:, n % 2, :], region[bank], parts[t][:, 0, oc, :], ALU.subtract)\
                    .then_inc(drained[bank], 1)

            def maxima(b, turn, f, a, h):
                g = h // GROUP
                for qt in range(T):
                    bank, _ = f[qt]
                    (wait_apart if CAUSAL[a] else wait)(dve, filled[bank], number(f[qt], turn) + 1)
                    dst = neg_max[:, g % 2, h % GROUP * T + qt:h % GROUP * T + qt + 1]
                    if CAUSAL[a]:
                        keys = (qt + 1) * P
                        v.tensor_tensor_reduce(region[bank][:, 0:keys], region[bank][:, 0:keys], causal[:, S - keys:S],
                                               1.0, -3e38, ALU.add, ALU.max, dst).then_inc(drained[bank], 1)
                    else:
                        v.tensor_reduce(dst, region[bank], AX_X, ALU.max).then_inc(drained[bank], 1)

            def max_rows(b, turn, f, a, g):
                wait(dve, filled["misc"], number(f[0], turn) + 1)
                groups = HEADS[a] // GROUP
                if g >= 2:
                    wait(dve, max_split[a], 4 * groups * b + 4 * (g - 1))
                elif a == 1:
                    wait(dve, max_split[0], 4 * (HEADS[0] // GROUP) * (b + 1))
                else:
                    wait(dve, max_split[1], 4 * (HEADS[1] // GROUP) * b)
                v.tensor_scalar(max_row[:, g % 2, :], misc[0:GROUP * T, 0:P], -1.0, None, ALU.mult)\
                    .then_inc(drained["misc"], 1)

            def normalise(b, turn, f, a, g):
                groups = HEADS[a] // GROUP
                d = WIDTH[a]
                wait(dve, filled["misc"], number(f[0], turn) + 1)
                turned = misc[:, :].rearrange("p (t k r) -> p t k r", t=T, k=GROUP)
                inv = inv_sum[:, :].rearrange("p (t k) -> p t k", t=T)
                v.reciprocal(inv, turned[:, :, :, d]).then_inc(sums_inverted[a], 1)
                wait(dve, sums_inverted[a], groups * b + g + 1)
                dst = heads[:, :, g * GROUP * d:(g + 1) * GROUP * d].rearrange("p t (k d) -> p t k d", d=d)
                v.tensor_tensor(dst, turned[:, :, :, 0:d], inv.unsqueeze(3).broadcast_to([P, T, GROUP, d]), ALU.mult)\
                    .then_inc(drained["misc"], 1)

            def attention_out(b, turn, f, half):
                (bank, _), = f
                wait(dve, filled[bank], number(f[0], turn) + 1)
                if half == 0:
                    wait(dve, mod_loaded, 16 * (b + 1))
                    wait(dve, res_made, 2 * b)
                rows = slice(2 * half, 2 * half + 2)
                v.tensor_tensor(x1[:, rows, :], region[bank].rearrange("p (t d) -> p t d", t=2),
                                mod_bc[:, 0:1, :].broadcast_to([P, 2, D]), ALU.mult).then_inc(drained[bank], 1)
                wait(dve, drained[bank], number(f[0], turn) + 1)
                v.tensor_tensor(x1[:, rows, :], x1[:, rows, :], x_in[:, rows, :], ALU.add).then_inc(x1_made, 1)

            def ffn_input(b, turn, f):
                for t in range(T):
                    wait(dve, normed_made[1], T * b + t + 1)
                    v.tensor_tensor(ffn_x[:, t, :], normed[1][:, t, :], mod_bc[:, 1, :], ALU.mult).then_inc(ffn_scaled, 1)
                for t in range(T):
                    wait(dve, ffn_scaled, T * b + t + 1)
                    v.tensor_tensor(ffn_x[:, t, :], ffn_x[:, t, :], mod_bc[:, 2, :], ALU.add).then_inc(ffn_x_made, 1)

            def bias_part(b, turn, f):
                wait(dve, gate_loaded, 48 * (b + 1))
                wait(dve, x1_made, 2 * (b + 1))
                for j in range(2):
                    v.tensor_tensor(b2_bc[:, j, :], b2_bc[:, j, :], gb_bc[:, :], ALU.mult).then_inc(bias_gated, 1)
                wait(dve, bias_gated, 2 * b + 2)
                for j in range(2):
                    v.tensor_tensor(x_res[:, 2 * j:2 * j + 2, :], x1[:, 2 * j:2 * j + 2, :],
                                    b2_bc[:, j:j + 1, :].broadcast_to([P, 2, D]), ALU.add).then_inc(res_made, 1)
                for j in range(2):
                    v.tensor_copy(b1_cur[:, j, :], b1_T[:, bass.ds(((b * 2 + j) % E) * FT, FT)]).then_inc(b1_made, 1)

            def ffn_sum(b, turn, f, mc):
                (bank, _), = f
                wait(dve, filled[bank], number(f[0], turn) + 1)
                v.tensor_tensor(expert_xT[:, mc, :], region[bank], ffn_xT[:, mc, :], ALU.add).then_inc(drained[bank], 1)

            def expert_out(b, turn, f, j):
                (bank, _), = f
                wait(dve, filled[bank], number(f[0], turn) + 1)
                wait(dve, y_stored[j], 16 * b + 1)
                v.tensor_tensor(y_out[:, j, :, :], region[bank].rearrange("p (t d) -> p t d", t=2),
                                gb_bc[:, :].unsqueeze(1).broadcast_to([P, 2, D]), ALU.mult).then_inc(drained[bank], 1)
                wait(dve, drained[bank], number(f[0], turn) + 1)
                wait(dve, res_made, 2 * (b + 1))
                v.tensor_tensor(y_out[:, j, :, :], y_out[:, j, :, :], x_res[:, 2 * j:2 * j + 2, :], ALU.add)\
                    .then_inc(y_made, 1)

            walk(dve, {"layernorm": layernorm, "to_features": to_features, "qk": qk, "maxima": maxima,
                       "max_rows": max_rows, "normalise": normalise, "attention_out": attention_out,
                       "ffn_input": ffn_input, "bias_part": bias_part, "ffn_sum": ffn_sum, "expert_out": expert_out})


_INS = ["L0_attn_in_features", "L0_attn_q_proj_weight", "L0_attn_k_proj_weight", "L0_attn_v_proj_weight",
        "L0_attn_o_proj_weight", "L0_ffn_ln_g", "L0_ffn_ln_b", "L0_ffn_wq", "L0_ffn_wk", "L0_ffn_wv", "L0_ffn_wo",
        "L0_ffn_w1", "L0_ffn_b1", "L0_ffn_w2", "L0_ffn_b2", "L0_c", "L0_wmod"]
_OUTS = [((8, 512, 256), "float32")]


def kernel(**inputs):
    import concourse.bacc as _bacc
    from concourse.bass_utils import run_bass_kernel_spmd as _run

    nc = _bacc.Bacc("TRN2", target_bir_lowering=False, num_devices=1)
    arrays, args = {}, []
    for name in _INS:
        a = np.ascontiguousarray(inputs[name])
        arrays[f"in_{name}_dram"] = a
        args.append(nc.dram_tensor(f"in_{name}_dram", a.shape, mybir.dt.from_np(a.dtype), kind="ExternalInput").ap())
    for i, (shape, dtype) in enumerate(_OUTS):
        dt = mybir.dt.from_np(np.dtype(dtype))
        args.append(nc.dram_tensor(f"out_{i}_dram", shape, dt, kind="ExternalOutput").ap())
    build(nc, *args)
    r = _run(nc, [arrays], core_ids=[0])
    return r.results[0]["out_0_dram"]
```

```python
from contextlib import ExitStack

import numpy as np

import concourse.bass as bass
from concourse import mybir

F32 = mybir.dt.float32
BF16 = mybir.dt.bfloat16
I32 = mybir.dt.int32
ALU = mybir.AluOpType
ACT = mybir.ActivationFunctionType
AX_X = mybir.AxisListType.X

P = 128
LN_EPS = 1e-5
GATE_MIN = 0.25
NEWTON = 3
ROOT_STEPS = 3 + 3 * NEWTON
MASKED = -1e30
LEAD = 7

HEADS = (16, 32)
WIDTH = (16, 8)
CAUSAL = (True, False)
Q_PARTS = ((0, 1, 2, 0, 1, 0), (0, 1, 2, 0, 1, 2, 0, 1, 2))
K_PARTS = ((0, 0, 0, 1, 1, 2), (0, 1, 2, 1, 2, 0, 2, 0, 1))
M_PARTS = 3
UNIT_HEADS = 8
GROUP = 4
BATCHES = 8
LOOPS = BATCHES - 2
UNITS = ((0, 1), (2, 3, 4, 5))
PRODUCT_ROWS = 96


def rows_of(a):
    return WIDTH[a] * len(Q_PARTS[a])


def runs(parts):
    out = []
    for g, part in enumerate(parts):
        if out and part == out[-1][1] + out[-1][2]:
            out[-1][2] += 1
        else:
            out.append([g, part, 1])
    return out



def attention(main, lead, beside=None):
    beside = beside or {}
    out = []
    group_maxima, probs, raw = [], [], []
    for p in range(max(len(main), len(lead))):
        head = lead[p] if p < len(lead) else None
        for k in range(GROUP):
            if p < len(main):
                off, a, s = main[p]
                out.append(("scores", off, a, s, k))
            if head:
                out.append(("maxima", *head, k))
        out += group_maxima
        group_maxima = []
        if head and head[2] % GROUP == GROUP - 1:
            group_maxima = [("max_rows", head[0], head[1], head[2] // GROUP)]
        out += probs
        probs = [("values", *main[p])] if p < len(main) else []
        out += [item for at, item in raw if at == p]
        if p < len(main) and main[p][2] % 4 == 3:
            off, a, s = main[p]
            raw.append((p + 3, ("normalise", off, a, s // 4)))
        out += beside.get(p, [])
    left = group_maxima + probs + beside.get("values", [])
    left += [item for at, item in raw if at >= max(len(main), len(lead))]
    return out + left + beside.get("end", [])


def project(a, off):
    return ([("v", off, a, half) for half in range(2)]
            + [("qk", off, a, t, oc) for t in range(2) for oc in range(2)])


def spread(plan, at, items, every=1):
    for n, item in enumerate(items):
        plan.setdefault(at + n * every, []).append(item)
    return at + len(items) * every


def experts(plan, off, at):
    plan.setdefault(at, []).extend([("expert_in", off, 0, f) for f in range(4)])
    plan.setdefault(at + 1, []).append(("load_expert_in", off, 1))
    for n in range(4):
        plan.setdefault(at + 1 + n // 2, []).append(("expert_out", off, 0, n))
    plan.setdefault(at + 3, []).append(("load_expert_out", off, 1))
    plan.setdefault(at + 4, []).extend([("expert_in", off, 1, f) for f in range(4)])
    return at + 5


def steps_of_attention(off, a):
    return [(off, a, s) for s in range(4 * HEADS[a] // GROUP)]


def heads_of_attention(off, a):
    return [(off, a, h) for h in range(HEADS[a])]


def sections():
    first = [("layernorm", 0)] + [("to_features", 0, c) for c in range(2)]
    second = [("layernorm", 1), ("ffn_input",), ("to_features", 1, 0), ("to_features", 1, 1),
              ("layernorm", 2), ("to_features", 2, 0), ("to_features", 2, 1)]
    of = lambda off, items: [(i[0], off, *i[1:]) for i in items]

    before = [("load_x", 0), ("load_residual", 0), ("load_mod", 0), *of(0, first), ("load_x", 1), *project(0, 0),
              ("stacks", 0, 0), ("stacks", 0, 1), *of(1, first), ("load_gate", 0)]
    ahead = heads_of_attention(0, 0) + heads_of_attention(1, 0)
    before += attention([], ahead[:LEAD])
    beside = {8: [("stacks", 1, 0)], 16: [("stacks", 1, 1), *project(0, 1)[:2]],
              20: [("head_features", 0, 0, 0)], 21: [("head_features", 0, 0, 1)],
              22: [("attention_out", 0, 0)], 23: [("attention_out", 0, 1), ("load_residual", 1)],
              24: of(0, second[:1]), 25: of(0, second[1:2]) + [("load_mod", 1)]}
    spread(beside, 0, project(0, 1)[2:])
    beside[26] = of(0, second[2:3])
    beside[27] = of(0, second[3:4])
    beside[28] = of(0, second[4:5])
    beside[30] = of(0, second[5:6])
    beside[31] = of(0, second[6:7])
    beside["values"] = project(1, 0)
    beside["end"] = [("head_features", 1, 0, 0), ("head_features", 1, 0, 1), ("stacks", 0, 2), ("stacks", 0, 3),
                     ("keep_v", 0), ("keep_x", 0), ("heads_turned", 1)]
    before += attention(steps_of_attention(0, 0) + steps_of_attention(1, 0), ahead[LEAD:], beside)
    before += attention([], heads_of_attention(0, 1)[:LEAD])

    n1, n0 = 4 * HEADS[1] // GROUP, 4 * HEADS[0] // GROUP
    beside = {}
    spread(beside, 0, [("load_x", 2), ("stacks", 0, 4), ("bias_part", 0)])
    spread(beside, 2, [("attention_out", 1, 0), ("attention_out", 1, 1), ("load_residual", 2)])
    beside[1].append(("layernorm", 2, 0))
    beside[1].append(("load_expert_in", 0, 0))
    beside[1].append(("load_expert_out", 0, 0))
    spread(beside, 4, of(2, first[1:]))
    spread(beside, 5, of(1, second[:2]) + [("load_mod", 2)])
    spread(beside, 6, project(0, 2))
    beside.setdefault(9, []).append(("stacks", 0, 5))
    spread(beside, 8, of(1, second[4:5]))
    spread(beside, 12, of(1, second[2:4]) + of(1, second[5:7]))
    spread(beside, 16, project(1, 1))
    beside.setdefault(17, []).append(("stacks", 2, 0))
    beside.setdefault(25, []).append(("stacks", 2, 1))
    x = n1
    spread(beside, x + 1, [("stacks", 1, 2), ("keep_v", 1)])
    spread(beside, x + 3, [("head_features", 0, 1, 0), ("head_features", 0, 1, 1), ("ffn_sum", 0, 0), ("ffn_sum", 0, 1),
                           ("keep_x", 1)])
    experts(beside, 0, x + 8)
    beside.setdefault(x + 9, []).append(("stacks", 1, 3))
    spread(beside, x + 13, [("expert_out", 0, 1, 0), ("expert_out", 0, 1, 1), ("expert_out", 0, 1, 2)])
    beside["end"] = [("head_features", 2, 0, 0), ("head_features", 2, 0, 1), ("expert_out", 0, 1, 3),
                     ("load_gate", 1), ("heads_turned", 2)]
    ahead = heads_of_attention(0, 1)[LEAD:] + heads_of_attention(2, 0) + heads_of_attention(1, 1)[:LEAD]
    loop = attention(steps_of_attention(0, 1) + steps_of_attention(2, 0), ahead, beside)

    beside = {}
    spread(beside, 0, [("stacks", 0, 4), ("bias_part", 0), ("attention_out", 1, 0), ("attention_out", 1, 1)])
    beside[1] += [("load_expert_in", 0, 0), ("load_expert_out", 0, 0)]
    spread(beside, 4, of(1, second))
    beside[9].append(("stacks", 0, 5))
    spread(beside, 11, project(1, 1))
    beside.setdefault(18, []).append(("stacks", 1, 2))
    beside.setdefault(25, []).append(("stacks", 1, 3))
    beside.setdefault(33, []).append(("stacks", 1, 4))
    beside.setdefault(41, []).append(("stacks", 1, 5))
    spread(beside, x, [("keep_v", 1)])
    spread(beside, x + 3, [("head_features", 0, 1, 0), ("head_features", 0, 1, 1), ("ffn_sum", 0, 0), ("ffn_sum", 0, 1),
                           ("keep_x", 1)])
    experts(beside, 0, x + 8)
    spread(beside, x + 13, [("expert_out", 0, 1, n) for n in range(4)])
    spread(beside, x + 18, [("load_gate", 1), ("load_expert_in", 1, 0), ("load_expert_out", 1, 0), ("bias_part", 1)])
    last = {}
    experts(last, 1, 0)
    beside["end"] = ([("head_features", 1, 1, 0), ("head_features", 1, 1, 1), ("ffn_sum", 1, 0), ("ffn_sum", 1, 1)]
                     + [item for p in sorted(last) for item in last[p]] + [("expert_out", 1, 1, n) for n in range(4)])
    ahead = heads_of_attention(0, 1)[LEAD:] + heads_of_attention(1, 1)
    after = attention(steps_of_attention(0, 1) + steps_of_attention(1, 1), ahead, beside)
    return (("before", before), ("loop", loop), ("after", after))


def banks_of(item):
    kind = item[0]
    if kind == "scores":
        _, _, _, s, k = item
        return ["scores%d" % ((GROUP * s + k) % 3)]
    if kind == "maxima":
        return ["max%d" % (item[4] % 2)]
    if kind in ("max_rows", "normalise"):
        return ["misc"]
    if kind == "values":
        return ["out"] if item[3] % 4 == 0 else []
    if kind in ("head_features", "attention_out"):
        return ["misc"]
    if kind in ("to_features", "qk", "v", "ffn_sum"):
        return ["side"]
    if kind == "expert_in":
        return [("side", "misc")[item[3] % 2]]
    if kind == "expert_out":
        return ["side"] if item[3] == 0 else []
    return []


BANKS = ("scores0", "scores1", "scores2", "max0", "max1", "out", "misc", "side")


def number_fills(plan):
    begun = dict.fromkeys(BANKS, 0)
    fills, per_loop = {}, {}
    for name, items in plan:
        count = dict.fromkeys(BANKS, 0)
        assert len(set(items)) == len(items)
        for item in items:
            fills[name, item] = []
            for bank in banks_of(item):
                fills[name, item].append((bank, begun[bank] + count[bank]))
                count[bank] += 1
        turns = (LOOPS if name == "loop" else 1)
        if name == "loop":
            per_loop = count
        for bank in BANKS:
            begun[bank] += turns * count[bank]
    return fills, per_loop


def build(nc, x, wq1, wk1, wv1, wo1, ln_g, ln_b, wq2, wk2, wv2, wo2, w1, b1, w2, b2, c, wmod, out):
    _, S, D = x.shape
    E, _, F = w1.shape
    T = S // P
    C = D // P
    FT = F // P
    EXP_TOK = S // 2
    assert S == 512 and D == 256 and T == 4 and C == 2 and EXP_TOK == 256

    plan = sections()
    fills, per_loop = number_fills(plan)

    q_dram = [nc.dram_tensor("q_parts0", (2, 3, D, S), BF16, kind="Internal").ap(),
              nc.dram_tensor("q_parts1", (2, C, 3, P, S), BF16, kind="Internal").ap()]
    k_dram = [nc.dram_tensor("k_parts0", (2, 3, D, S), BF16, kind="Internal").ap(),
              nc.dram_tensor("k_parts1", (2, C, 3, P, S), BF16, kind="Internal").ap()]
    zero_dram = nc.dram_tensor("zero_rows", (PRODUCT_ROWS - rows_of(1), UNIT_HEADS * S), BF16, kind="Internal").ap()
    mod_dram = nc.dram_tensor("mod_rows", (BATCHES, 4 * D), F32, kind="Internal").ap()

    with ExitStack() as ctx:
        def sb(name, shape, dt=F32):
            return ctx.enter_context(nc.sbuf_tensor(name, shape, dt))

        def psum(name, shape):
            return ctx.enter_context(nc.psum_tensor(name, shape, F32))

        def sem(name):
            return ctx.enter_context(nc.semaphore(name))

        region = {b: psum("bank_" + b, [P, 512])[:, :] for b in BANKS}
        outb, misc = region["out"], region["misc"]

        ident = sb("ident", [P, P])
        causal = sb("causal", [P, S])
        zeros = sb("zeros", [P, P], BF16)
        q_stack = [sb("q_stack%d" % n, [P, UNIT_HEADS, S], BF16) for n in range(3)]
        k_stack = [sb("k_stack%d" % n, [P, UNIT_HEADS, S], BF16) for n in range(3)]
        probs = [sb("probs%d" % n, [P, GROUP, S]) for n in range(2)]
        v_tile = [sb("v_tile%d" % a, [P, T, HEADS[a], WIDTH[a] + 1]) for a in range(2)]
        w_qkv = [[sb("w%s%d" % (n, a), [P, C, D]) for n in "qkv"] for a in range(2)]
        w_o = [sb("wo%d" % a, [P, C, D]) for a in range(2)]
        w_in = sb("w_in", [P, C, F])
        w_out = sb("w_out", [P, FT, D])
        v_next = sb("v_next", [P, T, HEADS[1], WIDTH[1]])
        x_in = sb("x_in", [P, T, D])
        x_again = sb("x_again", [P, T, D])
        x1 = sb("x1", [P, T, D])
        x_res = sb("x_res", [P, T, D])
        normed = [sb("normed%d" % n, [P, T, D]) for n in range(2)]
        ffn_x = normed[1]
        ffn_xT_next = sb("ffn_xT_next", [P, C, S])
        ffn_xT = sb("ffn_xT", [P, C, S])
        act_T = sb("act_T", [P, C, S])
        parts = [sb("parts%s" % n, [P, 3, C, S], BF16) for n in "qk"]
        rest = sb("rest", [P, 2, S])
        neg_max = sb("neg_max", [P, 2, GROUP * T])
        max_row = sb("max_row", [GROUP * T, 2, P])
        max_rest = sb("max_rest", [GROUP * T, 2, P])
        max_parts = sb("max_parts", [GROUP * T, 2, M_PARTS, P], BF16)
        out_raw = sb("out_raw", [P, 2, S])
        inv_sum = sb("inv_sum", [P, T * GROUP])
        heads = sb("heads", [P, T, D])
        heads_T = sb("heads_T", [P, C, S])
        expert_xT = sb("expert_xT", [P, C, S])
        hidden_T = sb("hidden_T", [P, FT, EXP_TOK])
        y_out = sb("y_out", [P, 2, 2, D])
        mod_bc = sb("mod_bc", [P, 3, D])
        gb_bc = sb("gb_bc", [P, D])
        b2_bc = sb("b2_bc", [P, 2, D])
        mod_T = sb("mod_T", [P, 2 * C, BATCHES])
        mod_cur = sb("mod_cur", [P, 2 * C])
        b1_T = sb("b1_T", [P, E * FT])
        b1_cur = sb("b1_cur", [P, 2, FT])
        lng_T = sb("lng_T", [P, C])
        lnb_T = sb("lnb_T", [P, C])
        stats = sb("stats", [P, 3, T, 6])
        mean_var = sb("mean_var", [P, 3, T, 2])
        rstd = sb("rstd", [P, 3, T])
        root = sb("root", [P, 3, 2, T])
        c_T = sb("c_T", [P, C, BATCHES])
        silu = sb("silu", [P, 3, C, BATCHES])
        mod_row = hidden_T[0:BATCHES, 0:4, :]
        gate_tmp = hidden_T[0:BATCHES, 4:8, :].rearrange("b (k i) d -> b k i d", k=2)
        def stage(tile, at, shape):
            n = shape[0] * shape[1]
            flat_tile = tile[:, :, :].rearrange("p a s -> p (a s)")[:, 2 * at:2 * (at + n)].bitcast(F32)
            return flat_tile.rearrange("p (c d) -> p c d", c=shape[0])

        stage_w = [stage(q_stack[i % 3], C * D * (i // 3), (C, D)) for i in range(4)]
        stage_w2 = [stage(q_stack[i], C * D, (C, D)) for i in (1, 2)]
        stage_b1 = stage(q_stack[0], 2 * C * D, (1, P))[:, 0, :]
        stage_mod = probs[0][:, :, :].rearrange("p a s -> p (a s)")[:, 0:C * 768].rearrange("p (c n) -> p c n", c=C)
        stage_mod2 = probs[1][:, :, :].rearrange("p a s -> p (a s)")[:, 0:C * 768].rearrange("p (c n) -> p c n", c=C)

        filled = {b: sem("filled_" + b) for b in BANKS}
        drained = {b: sem("drained_" + b) for b in BANKS}
        const_made = sem("const_made")
        small_in = sem("small_in")
        weights_in = sem("weights_in")
        mod_in = sem("mod_in")
        silu_step = sem("silu_step")
        silu_exp = sem("silu_exp")
        pro_filled = sem("pro_filled")
        pro_drained = sem("pro_drained")
        gate_step = sem("gate_step")
        mod_rows_made = sem("mod_rows_made")
        mod_stored = sem("mod_stored")
        stage_done = sem("stage_done")
        perm_done = sem("perm_done")
        ones_made = sem("ones_made")
        waits_passed = sem("waits_passed")
        x_loaded = sem("x_loaded")
        mod_loaded = sem("mod_loaded")
        gate_loaded = sem("gate_loaded")
        residual_loaded = sem("residual_loaded")
        v_kept = sem("v_kept")
        x_kept = sem("x_kept")
        mod_cur_made = sem("mod_cur_made")
        stats_made = [sem("stats_made%d" % n) for n in range(3)]
        moments_made = [sem("moments_made%d" % n) for n in range(3)]
        rstd_made = [sem("rstd_made%d" % n) for n in range(3)]
        normed_made = [sem("normed_made%d" % n) for n in range(3)]
        features_made = [sem("features_made%d" % n) for n in range(3)]
        top_made = [sem("top_made%d" % a) for a in range(2)]
        second_made = [sem("second_made%d" % a) for a in range(2)]
        split_made = [sem("split_made%d" % a) for a in range(2)]
        parts_stored = [sem("parts_stored%d" % a) for a in range(2)]
        stack_loaded = [sem("stack_loaded%d" % u) for u in range(6)]
        max_split = [sem("max_split%d" % a) for a in range(2)]
        max_stored = [[sem("max_stored%d%d" % (a, n)) for n in range(2)] for a in range(2)]
        masked_made = sem("masked_made")
        values_done = [sem("values_done%d" % a) for a in range(2)]
        sums_inverted = [sem("sums_inverted%d" % a) for a in range(2)]
        x1_gated = sem("x1_gated")
        x1_made = sem("x1_made")
        ffn_scaled = sem("ffn_scaled")
        ffn_x_made = sem("ffn_x_made")
        bias_gated = sem("bias_gated")
        res_made = sem("res_made")
        w_in_loaded = sem("w_in_loaded")
        w_out_loaded = sem("w_out_loaded")
        b1_made = sem("b1_made")
        y_made = sem("y_made")
        y_stored = [sem("y_stored%d" % j) for j in range(2)]

        w_view = [(w, i) for i, w in enumerate((wq1, wk1, wv1, wo1))]

        def number(fill, turn):
            bank, n = fill
            return n if turn is None else turn * per_loop[bank] + n

        def wait(eng, semaphore, value):
            if isinstance(value, int) and value <= 0:
                return
            eng.wait_ge(semaphore, value)

        def wait_apart(eng, semaphore, value):
            wait(eng, semaphore, value)
            if not isinstance(value, int):
                eng.sem_inc(waits_passed, 1)

        def walk(eng, share):
            for name, items in plan:
                if name == "loop":
                    with eng.Fori(0, LOOPS) as turn:
                        for item in items:
                            if item[0] in share:
                                share[item[0]](turn + item[1] if item[1] else turn, turn, fills[name, item], *item[2:])
                else:
                    for item in items:
                        if item[0] in share:
                            share[item[0]](item[1] + (LOOPS if name == "after" else 0), None, fills[name, item], *item[2:])

        def previous(a, b):
            if a == 0:
                return (1, b - 1) if not isinstance(b, int) or b > 1 else (0, b)
            return (0, b + 2) if not isinstance(b, int) or b + 2 <= BATCHES else (1, b)

        def buffer_of(u, b):
            return (u + 1) % 3 if isinstance(b, int) and b == BATCHES - 1 and u >= 2 else u % 3

        def buffer_free(u, b):
            per = 2 * T
            one, all_one = values_done[1], steps_of[1]
            if u < 2:
                if isinstance(b, int) and b < 2:
                    return values_done[0], (2 * per) * (b - 1) + per * (u + 1)
                return one, all_one * (b - 2) + per * (u + 2)
            if isinstance(b, int) and b == BATCHES - 1:
                return one, all_one * (b - 1) + per * u if u < 5 else all_one * b + per
            if u == 2:
                return one, all_one * b
            if u == 5:
                return one, all_one * b + per
            return values_done[0], 2 * per * (b + 1) + per * (u - 2)

        def unit_of(a, h):
            return UNITS[a][h // UNIT_HEADS]

        stack_dmas = [len(runs(Q_PARTS[a])) + len(runs(K_PARTS[a])) for a in (0, 0, 1, 1, 1, 1)]
        stack_dmas[3] += 1
        stack_dmas[4] += 1
        steps_of = [T * h // GROUP for h in HEADS]

        block = ctx.enter_context(nc.Block())

        @block.sync
        def _(sp):
            for j in range(2):
                sp.sem_inc(y_stored[j], 1)
            sp.sem_inc(y_made, 1)
            with nc.allow_non_contiguous_dma("a few kilobytes"):
                for cc in range(C):
                    sp.dma_start(c_T[:, cc, :], c[:, cc * P:(cc + 1) * P].rearrange("b p -> p b")).then_inc(small_in, 16)
                sp.dma_start(lng_T[:, :], ln_g.rearrange("(c p) -> p c", p=P)).then_inc(small_in, 16)
                sp.dma_start(lnb_T[:, :], ln_b.rearrange("(c p) -> p c", p=P)).then_inc(small_in, 16)
            sp.dma_start(stage_mod, wmod[:, 0:768].rearrange("(c p) n -> p c n", p=P)).then_inc(mod_in, 16)
            sp.dma_start(stage_mod2, wmod[:, 768:1536].rearrange("(c p) n -> p c n", p=P)).then_inc(mod_in, 16)
            sp.wait_ge(ones_made, 4)
            sp.dma_start(zero_dram[:, :], k_stack[0][0:PRODUCT_ROWS - rows_of(1), :, :].rearrange("p h s -> p (h s)"))\
              .then_inc(mod_stored, 16)
            sp.dma_start(stage_b1[0:E * FT, :], b1.rearrange("e (f p) -> (e f) p", p=P)).then_inc(weights_in, 16)
            for w, i in w_view:
                sp.dma_start(stage_w[i], w.rearrange("(c p) n -> p c n", p=P)).then_inc(weights_in, 16)
            for w, st in ((wq2, stage_w2[0]), (wk2, stage_w2[1]), (wv2, w_qkv[1][2][:, :, :]), (wo2, w_o[1][:, :, :])):
                sp.dma_start(st, w.rearrange("(c p) n -> p c n", p=P)).then_inc(weights_in, 16)
            sp.wait_ge(mod_rows_made, 6)
            sp.dma_start(mod_dram[:, :], mod_row[:, :, :].rearrange("b v d -> b (v d)")).then_inc(mod_stored, 16)
            sp.wait_ge(mod_stored, 32)

            def load_x(b, turn, f):
                wait_apart(sp, normed_made[0], T * b)
                sp.dma_start(x_in[:, :, :], x[b].rearrange("(t p) d -> p t d", p=P)).then_inc(x_loaded, 16)

            def load_residual(b, turn, f):
                wait_apart(sp, x1_made, 2 * b)
                sp.dma_start(x_again[:, :, :], x[b].rearrange("(t p) d -> p t d", p=P)).then_inc(residual_loaded, 16)

            def load_mod(b, turn, f):
                wait_apart(sp, ffn_x_made, T * b)
                sp.dma_start(mod_bc[:, :, :].rearrange("p v d -> p (v d)"),
                             mod_dram[b, 0:3 * D].partition_broadcast(P)).then_inc(mod_loaded, 16)

            def load_gate(b, turn, f):
                wait_apart(sp, y_made, 2 * b + 1)
                sp.dma_start(gb_bc[:, :], mod_dram[b, 3 * D:4 * D].partition_broadcast(P)).then_inc(gate_loaded, 16)
                for j in range(2):
                    sp.dma_start(b2_bc[:, j, :], b2[(b * 2 + j) % E].partition_broadcast(P)).then_inc(gate_loaded, 16)

            hidden_fill = {}

            def expert_in(b, turn, f, j, n):
                hidden_fill[0] = f[0]

            def load_expert_in(b, turn, f, j):
                e = (b * 2 + j) % E
                if j == 0:
                    wait_apart(sp, y_made, 2 * b + 1)
                else:
                    bank, _ = hidden_fill[0]
                    wait_apart(sp, filled[bank], number(hidden_fill[0], turn) + 1)
                sp.dma_start(w_in[:, :, :], w1[e].rearrange("(c p) n -> p c n", p=P)).then_inc(w_in_loaded, 16)

            def load_expert_out(b, turn, f, j):
                e = (b * 2 + j) % E
                wait_apart(sp, y_made, 2 * b + j + 1)
                sp.dma_start(w_out[:, :, :], w2[e].rearrange("(f p) n -> p f n", p=P)).then_inc(w_out_loaded, 16)

            def qk(b, turn, f, a, t, oc):
                n = 2 * t + oc
                if n == 0 and not (isinstance(b, int) and b < 2):
                    for u in UNITS[a]:
                        wait_apart(sp, stack_loaded[u], 16 * stack_dmas[u] * (b - 1))
                wait_apart(sp, split_made[a], 4 * b + n + 1)
                dram = (q_dram, k_dram)[t][a][b % 2]
                dst = dram[:, oc * P:(oc + 1) * P, :] if a == 0 else dram[oc]
                sp.dma_start(dst.rearrange("i p s -> p i s"), parts[t][:, :, oc, :]).then_inc(parts_stored[a], 16)

            def stacks(b, turn, f, u):
                a = 0 if u in UNITS[0] else 1
                d = WIDTH[a]
                buf = buffer_of(u, b)
                wait_apart(sp, parts_stored[a], 16 * 4 * (b + 1))
                wait_apart(sp, *buffer_free(u, b))
                at = u % 2 * UNIT_HEADS * S
                for dram, stack, order in ((q_dram, q_stack, Q_PARTS[a]), (k_dram, k_stack, K_PARTS[a])):
                    src = dram[0][b % 2] if a == 0 else dram[1][b % 2, (u - 2) // 2]
                    src = src.rearrange("i (d h) s -> (i d) (h s)", d=d)[:, at:at + UNIT_HEADS * S]
                    dst = stack[buf][:, :, :].rearrange("p h s -> p (h s)")
                    for g, part, n in runs(order):
                        sp.dma_start(dst[g * d:(g + n) * d, :], src[part * d:(part + n) * d, :])\
                          .then_inc(stack_loaded[u], 16)
                if u in (3, 4):
                    sp.dma_start(k_stack[buf][rows_of(1):PRODUCT_ROWS, :, :].rearrange("p h s -> p (h s)"), zero_dram[:, :])\
                      .then_inc(stack_loaded[u], 16)

            def max_rows(b, turn, f, a, g):
                groups = HEADS[a] // GROUP
                u = unit_of(a, g * GROUP)
                r, h = P - M_PARTS, g * GROUP % UNIT_HEADS
                wait_apart(sp, max_split[a], 4 * groups * b + 4 * g + 4)
                for m in range(M_PARTS):
                    dst = q_stack[buffer_of(u, b)][r + m:r + m + 1, h:h + GROUP, :].rearrange("p h (q t) -> p (h q) t", t=P)
                    sp.dma_start(dst, max_parts[:, g % 2, m, :]).then_inc(max_stored[a][g % 2], 16)

            def expert_out(b, turn, f, j, n):
                if n < 3:
                    return
                wait_apart(sp, y_made, 2 * b + j + 2)
                half = out[b].rearrange("(j t p) d -> j p t d", j=2, p=P)[j]
                sp.dma_start(half, y_out[:, j, :, :]).then_inc(y_stored[j], 16)

            walk(sp, {"load_x": load_x, "load_residual": load_residual, "load_mod": load_mod, "load_gate": load_gate,
                      "load_expert_in": load_expert_in, "load_expert_out": load_expert_out, "qk": qk,
                      "stacks": stacks, "max_rows": max_rows, "expert_in": expert_in, "expert_out": expert_out})
            for j in range(2):
                sp.wait_ge(y_stored[j], 16 * BATCHES + 1)

        @block.gpsimd
        def _(pool):
            pool.memset(ident[:, :], 0.0).then_inc(const_made, 1)
            pool.memset(causal[:, :], 0.0).then_inc(const_made, 1)
            pool.memset(zeros[:, :], 0.0).then_inc(const_made, 1)
            for a in range(2):
                pool.memset(v_tile[a][:, :, :, WIDTH[a]:WIDTH[a] + 1], 1.0).then_inc(const_made, 1)
            pool.wait_ge(const_made, 5)
            pool.affine_select(out=ident[:, :], in_=ident[:, :], compare_op=ALU.not_equal, fill=1.0, base=0,
                               pattern=[[-1, P]], channel_multiplier=1).then_inc(const_made, 1)
            pool.affine_select(out=causal[:, S - P:S], in_=causal[:, S - P:S], compare_op=ALU.is_ge, fill=MASKED,
                               base=0, pattern=[[-1, P]], channel_multiplier=1).then_inc(const_made, 1)
            pool.memset(k_stack[0][:, :, :], 1.0).then_inc(ones_made, 1)
            for n in range(1, 3):
                pool.memset(k_stack[n][:, :, :], 1.0).then_inc(ones_made, 1)
            pool.wait_ge(ones_made, 3)
            for n in range(3):
                pool.memset(k_stack[n][0:P - M_PARTS, :, :], 0.0).then_inc(ones_made, 1)
            pool.wait_ge(pro_drained, 9)
            pool.wait_ge(perm_done, 4)
            for n in range(3):
                pool.memset(q_stack[n][:, :, :], 0.0).then_inc(ones_made, 1)

            def qk(b, turn, f, a, t, oc):
                n = 4 * b + 2 * t + oc
                buf = (2 * t + oc) % 2
                bank, _ = f[0]
                wait_apart(pool, drained[bank], number(f[0], turn) + 1)
                if t == 0 and oc == 0:
                    other, count = previous(a, b)
                    wait_apart(pool, parts_stored[other], 64 * count)
                pool.tensor_copy(parts[t][:, 1, oc, :], rest[:, buf, :]).then_inc(second_made[a], 1)
                wait(pool, second_made[a], n + 1)
                pool.tensor_tensor(parts[t][:, 2, oc, :], rest[:, buf, :], parts[t][:, 1, oc, :], ALU.subtract)\
                    .then_inc(split_made[a], 1)

            def max_rows(b, turn, f, a, g):
                groups = HEADS[a] // GROUP
                n = 4 * groups * b + 4 * g
                buf = g % 2
                wait(pool, drained["misc"], number(f[0], turn) + 1)
                per = [48 * (h // GROUP // 2) for h in HEADS]
                if g >= 2:
                    wait_apart(pool, max_stored[a][buf], per[a] * b + 48 * (g // 2))
                else:
                    other, count = previous(a, b)
                    wait_apart(pool, max_stored[other][buf], per[other] * count)
                pool.tensor_copy(max_parts[:, buf, 0, :], max_row[:, buf, :]).then_inc(max_split[a], 1)
                wait(pool, max_split[a], n + 1)
                pool.tensor_tensor(max_rest[:, buf, :], max_row[:, buf, :], max_parts[:, buf, 0, :], ALU.subtract)\
                    .then_inc(max_split[a], 1)
                wait_apart(pool, max_split[a], n + 2)
                pool.tensor_copy(max_parts[:, buf, 1, :], max_rest[:, buf, :]).then_inc(max_split[a], 1)
                wait(pool, max_split[a], n + 3)
                pool.tensor_tensor(max_parts[:, buf, 2, :], max_rest[:, buf, :], max_parts[:, buf, 1, :],
                                   ALU.subtract).then_inc(max_split[a], 1)

            def scores(b, turn, f, a, s, k):
                if not CAUSAL[a] or k < GROUP - 1:
                    return
                bank, _ = f[0]
                wait_apart(pool, drained[bank], number(f[0], turn) + 1)
                q0 = (s % T) * P
                tile = probs[s % 2][:, :, q0:q0 + P]
                pool.affine_select(out=tile, in_=tile, compare_op=ALU.is_ge, fill=0.0, base=0,
                                   pattern=[[0, GROUP], [1, P]], channel_multiplier=-1).then_inc(masked_made, 1)

            walk(pool, {"qk": qk, "max_rows": max_rows, "scores": scores})

        @block.scalar
        def _(act):
            act.wait_ge(small_in, 64)
            nc.scalar.activation(silu[:, 0, :, :], c_T[:, :, :], ACT.Exp, scale=-1.0).then_inc(silu_exp, 1)

            def qk(b, turn, f, a, t, oc):
                (bank, n), = f
                wait(act, filled[bank], number(f[0], turn) + 1)
                if t == 0 and oc == 0:
                    other, count = previous(a, b)
                    wait(act, parts_stored[other], 64 * count)
                nc.scalar.activation(parts[t][:, 0, oc, :], region[bank], ACT.Copy).then_inc(top_made[a], 1)

            def v(b, turn, f, a, half):
                (bank, n), = f
                wait(act, filled[bank], number(f[0], turn) + 1)
                d = WIDTH[a]
                dst = v_tile[0] if a == 0 else v_next
                nc.scalar.activation(dst[:, 2 * half:2 * half + 2, :, 0:d],
                                     region[bank].rearrange("p (t h d) -> p t h d", t=2, d=d), ACT.Copy)\
                    .then_inc(drained[bank], 1)

            def to_features(b, turn, f, n, cc):
                if n == 0:
                    return
                (bank, _), = f
                wait(act, filled[bank], number(f[0], turn) + 1)
                if n == 1:
                    nc.scalar.activation(ffn_xT_next[:, cc, :], region[bank], ACT.Copy).then_inc(drained[bank], 1)
                else:
                    nc.scalar.activation(act_T[:, cc, :], region[bank], ACT.Identity, bias=lnb_T[:, cc:cc + 1],
                                         scale=lng_T[:, cc:cc + 1]).then_inc(drained[bank], 1)

            def scores(b, turn, f, a, s, k):
                q0 = (s % T) * P if CAUSAL[a] else 0
                if k == 0:
                    if s >= 2:
                        wait(act, values_done[a], steps_of[a] * b + s - 1)
                    else:
                        other, count = previous(a, b)
                        wait(act, values_done[other], steps_of[other] * count - 1 + s)
                bank, _ = f[0]
                wait(act, filled[bank], number(f[0], turn) + 1)
                nc.scalar.activation(probs[s % 2][:, k, q0:S], region[bank][:, q0:S], ACT.Exp,
                                     scale=float(WIDTH[a]) ** -0.5).then_inc(drained[bank], 1)

            def values(b, turn, f, a, s):
                if s % T != T - 1:
                    return
                g = s // T
                steps = T * HEADS[a] // GROUP
                wait(act, values_done[a], steps * b + s + 1)
                groups = [h // GROUP for h in HEADS]
                if g >= 2:
                    wait(act, sums_inverted[a], groups[a] * b + g - 1)
                else:
                    other, count = previous(a, b)
                    wait(act, sums_inverted[other], groups[other] * count)
                nc.scalar.activation(out_raw[:, g % 2, :], outb[:, :], ACT.Copy).then_inc(drained["out"], 1)

            def head_features(b, turn, f, a, cc):
                (bank, _), = f
                wait(act, filled[bank], number(f[0], turn) + 1)
                nc.scalar.activation(heads_T[:, cc, :], region[bank], ACT.Copy).then_inc(drained[bank], 1)

            def expert_in(b, turn, f, j, n):
                (bank, _), = f
                wait(act, filled[bank], number(f[0], turn) + 1)
                if n == 0:
                    wait(act, b1_made, 2 * (b + 1))
                    if j == 1:
                        wait(act, y_made, 2 * b + 2)
                for k in range(2):
                    ins = nc.scalar.activation(hidden_T[:, 2 * n + k, :], region[bank][:, k * 256:(k + 1) * 256],
                                               ACT.Gelu, bias=b1_cur[:, j, 2 * n + k:2 * n + k + 1])
                ins.then_inc(drained[bank], 1)

            def keep_v(b, turn, f):
                wait(act, values_done[1], steps_of[1] * b)
                nc.scalar.activation(v_tile[1][:, :, :, 0:WIDTH[1]], v_next[:, :, :, :], ACT.Copy).then_inc(v_kept, 1)

            def ffn_sum(b, turn, f, mc):
                sum_fill[0] = f[0]

            sum_fill = {}

            def keep_x(b, turn, f):
                if sum_fill:
                    bank, _ = sum_fill[0]
                    wait(act, drained[bank], number(sum_fill[0], turn) + 1)
                nc.scalar.activation(ffn_xT[:, :, :], ffn_xT_next[:, :, :], ACT.Copy).then_inc(x_kept, 1)

            walk(act, {"keep_v": keep_v, "keep_x": keep_x, "ffn_sum": ffn_sum,
                       "qk": qk, "v": v, "to_features": to_features, "scores": scores, "values": values,
                       "head_features": head_features, "expert_in": expert_in})

        @block.tensor
        def _(pe):
            pe.wait_ge(const_made, 7)
            for k in range(4):
                pe.matmul(outb[:, k * P:(k + 1) * P], zeros[:, :], zeros[:, :], start=True, stop=True)
            maxb = (region["max0"], region["max1"])
            pe.wait_ge(weights_in, 16 * 9)
            n = 0
            for i in range(4):
                for ic in range(C):
                    if n >= 2:
                        pe.wait_ge(pro_drained, n - 1)
                    for oc in range(C):
                        ins = pe.transpose(maxb[n % 2][:, oc * P:(oc + 1) * P], stage_w[i][:, oc, ic * P:(ic + 1) * P],
                                           ident[:, :])
                    ins.then_inc(pro_filled, 1)
                    n += 1
            pe.wait_ge(pro_drained, n - 1)
            pe.transpose(maxb[0][:, 0:E * FT], stage_b1[0:E * FT, :], ident[0:E * FT, 0:E * FT]).then_inc(pro_filled, 1)
            pe.wait_ge(mod_in, 32)
            pe.wait_ge(silu_step, 3)
            stages = (stage_mod, stage_mod2)
            for bank, lo, hi in ((region["scores0"], 512, 768), (region["scores1"], 768, 1280), (region["scores2"], 1280, 1536)):
                st, o = (stages[0], 0) if hi <= 768 else (stages[1], 768)
                for cc in range(C):
                    ins = pe.matmul(bank[0:BATCHES, 0:hi - lo], silu[:, 0, cc, :], st[:, cc, lo - o:hi - o],
                                    start=(cc == 0), stop=(cc == C - 1))
                ins.then_inc(pro_filled, 1)
            for k in range(2 * C):
                for cc in range(C):
                    ins = pe.matmul(region["side"][:, k * BATCHES:(k + 1) * BATCHES], stages[0][:, cc, k * P:(k + 1) * P],
                                    silu[:, 0, cc, :], start=(cc == 0), stop=(cc == C - 1))
            ins.then_inc(pro_filled, 1)
            pe.wait_ge(pro_drained, 9)
            pe.wait_ge(mod_rows_made, 6)
            pe.wait_ge(perm_done, 4)
            pe.wait_ge(ones_made, 9)

            def start_fill(f, turn):
                bank, _ = f
                wait(pe, drained[bank], number(f, turn))

            def to_features(b, turn, f, n, cc):
                (bank, _), = f
                start_fill(f[0], turn)
                if n == 1:
                    wait(pe, ffn_x_made, T * (b + 1))
                    src = ffn_x
                else:
                    wait(pe, normed_made[n], T * (b + 1))
                    src = normed[n % 2]
                for t in range(T):
                    ins = pe.transpose(region[bank][:, t * P:(t + 1) * P], src[:, t, cc * P:(cc + 1) * P], ident[:, :])
                ins.then_inc(filled[bank], 1)

            def wait_drained(fs, turn, into=None):
                for bank, n in {bank: (bank, n) for bank, n in sorted(fs)}.values():
                    if bank != into:
                        wait(pe, drained[bank], number((bank, n), turn) + 1)

            last_features = {}

            def to_features_noted(b, turn, f, n, cc):
                to_features(b, turn, f, n, cc)
                last_features[n, cc] = f[0]


            def qk(b, turn, f, a, t, oc):
                (bank, _), = f
                start_fill(f[0], turn)
                for cc in range(C):
                    ins = pe.matmul(region[bank], w_qkv[a][t][:, cc, oc * P:(oc + 1) * P], act_T[:, cc, :],
                                    start=(cc == 0), stop=(cc == C - 1))
                ins.then_inc(filled[bank], 1)

            def v(b, turn, f, a, half):
                (bank, _), = f
                if half == 0:
                    wait_drained([last_features[2 * a, cc] for cc in range(C)], turn, bank)
                start_fill(f[0], turn)
                for k in range(2):
                    t = 2 * half + k
                    for cc in range(C):
                        ins = pe.matmul(region[bank][:, k * D:(k + 1) * D], act_T[:, cc, t * P:(t + 1) * P],
                                        w_qkv[a][2][:, cc, :], start=(cc == 0), stop=(cc == C - 1))
                ins.then_inc(filled[bank], 1)

            last_maxima = {}

            def maxima(b, turn, f, a, h, qt):
                u = unit_of(a, h)
                buf, hh, r = buffer_of(u, b), h % UNIT_HEADS, P - M_PARTS
                if hh == 0 and qt == 0:
                    wait(pe, stack_loaded[u], 16 * stack_dmas[u] * (b + 1))
                bank, _ = f[0]
                keys = (qt + 1) * P if CAUSAL[a] else S
                start_fill(f[0], turn)
                pe.matmul(region[bank][:, 0:keys], q_stack[buf][0:r, hh, qt * P:(qt + 1) * P],
                          k_stack[buf][0:r, hh, 0:keys], start=True, stop=True).then_inc(filled[bank], 1)
                last_maxima[0] = f[0]

            def max_rows(b, turn, f, a, g):
                bank, _ = last_maxima[0]
                wait(pe, drained[bank], number(last_maxima[0], turn) + 1)
                start_fill(f[0], turn)
                pe.transpose(misc[0:GROUP * T, 0:P], neg_max[:, g % 2, :], ident[:, :]).then_inc(filled["misc"], 1)

            def scores(b, turn, f, a, s, k):
                g, kt = s // T, s % T
                u = unit_of(a, g * GROUP)
                buf = buffer_of(u, b)
                q0 = kt * P if CAUSAL[a] else 0
                if kt == 0 and k == 0:
                    groups = HEADS[a] // GROUP
                    wait(pe, max_stored[a][g % 2], 48 * (groups // 2) * b + 48 * (g // 2 + 1))
                bank, _ = f[0]
                start_fill(f[0], turn)
                h = (g * GROUP + k) % UNIT_HEADS
                pe.matmul(region[bank][:, q0:S], k_stack[buf][:, h, kt * P:(kt + 1) * P], q_stack[buf][:, h, q0:S],
                          start=True, stop=True).then_inc(filled[bank], 1)
                last_scores[s % 2] = f[0]

            last_scores = {}

            def values(b, turn, f, a, s):
                g, kt = s // T, s % T
                q0 = kt * P if CAUSAL[a] else 0
                if kt == 0:
                    start_fill(f[0], turn)
                    if a == 1 and s == 0:
                        wait(pe, v_kept, b + 1)
                bank, _ = last_scores[s % 2]
                wait(pe, drained[bank], number(last_scores[s % 2], turn) + 1)
                if CAUSAL[a]:
                    wait(pe, masked_made, T * HEADS[a] // GROUP * b + s + 1)
                for k in range(GROUP):
                    ins = pe.matmul(outb[32 * k:32 * k + WIDTH[a] + 1, q0:S], v_tile[a][:, kt, g * GROUP + k, :],
                                    probs[s % 2][:, k, q0:S], start=(kt == 0), stop=(kt == T - 1),
                                    skip_group_check=True)
                ins.then_inc(values_done[a], 1)

            def normalise(b, turn, f, a, g):
                wait(pe, drained["out"], out_number(b, a, g) + 1)
                start_fill(f[0], turn)
                for t in range(T):
                    ins = pe.transpose(misc[:, t * P:(t + 1) * P], out_raw[:, g % 2, t * P:(t + 1) * P], ident[:, :])
                ins.then_inc(filled["misc"], 1)

            def out_number(b, a, g):
                first, second = (h // GROUP for h in HEADS)
                other, count = previous(a, b)
                if a == 0:
                    return first * b + (second * count if other == 1 else 0) + g
                return second * b + first * (count if other == 0 else BATCHES) + g

            def head_features(b, turn, f, a, cc):
                (bank, _), = f
                start_fill(f[0], turn)
                if cc == 0:
                    wait(pe, drained["misc"], number(last_misc[0], turn) + 1)
                for t in range(T):
                    ins = pe.transpose(region[bank][:, t * P:(t + 1) * P], heads[:, t, cc * P:(cc + 1) * P], ident[:, :])
                ins.then_inc(filled[bank], 1)
                last_heads[cc] = f[0]

            last_heads = {}
            last_misc = {}

            def normalise_noted(b, turn, f, a, g):
                normalise(b, turn, f, a, g)
                last_misc[0] = f[0]

            def heads_ready(turn, into=None):
                wait_drained(last_heads.values(), turn, into)

            def heads_turned(b, turn, f):
                heads_ready(turn)
                last_heads.clear()

            def attention_out(b, turn, f, half):
                (bank, _), = f
                heads_ready(turn, bank)
                start_fill(f[0], turn)
                for k in range(2):
                    t = 2 * half + k
                    for cc in range(C):
                        ins = pe.matmul(region[bank][:, k * D:(k + 1) * D], heads_T[:, cc, t * P:(t + 1) * P],
                                        w_o[0][:, cc, :], start=(cc == 0), stop=(cc == C - 1))
                ins.then_inc(filled[bank], 1)

            def ffn_sum(b, turn, f, mc):
                (bank, _), = f
                heads_ready(turn, bank)
                start_fill(f[0], turn)
                for cc in range(C):
                    ins = pe.matmul(region[bank], w_o[1][:, cc, mc * P:(mc + 1) * P], heads_T[:, cc, :],
                                    start=(cc == 0), stop=(cc == C - 1))
                ins.then_inc(filled[bank], 1)
                last_sum[mc] = f[0]

            last_sum = {}
            last_hidden = {}

            def expert_in(b, turn, f, j, n):
                (bank, _), = f
                if n == 0:
                    wait(pe, w_in_loaded, 16 * (2 * b + j + 1))
                    if j == 0:
                        wait_drained(last_sum.values(), turn, bank)
                start_fill(f[0], turn)
                for k in range(2):
                    ft = 2 * n + k
                    for cc in range(C):
                        ins = pe.matmul(region[bank][:, k * EXP_TOK:(k + 1) * EXP_TOK],
                                        w_in[:, cc, ft * P:(ft + 1) * P],
                                        expert_xT[:, cc, j * EXP_TOK:(j + 1) * EXP_TOK],
                                        start=(cc == 0), stop=(cc == C - 1))
                ins.then_inc(filled[bank], 1)
                last_hidden[n] = f[0]

            def expert_out(b, turn, f, j, n):
                if n == 0:
                    start_fill(f[0], turn)
                    last_out[0] = f[0]
                    wait(pe, w_out_loaded, 16 * (2 * b + j + 1))
                    wait_drained(last_hidden.values(), turn, f[0][0])
                bank, _ = last_out[0]
                k, part = n // 2, n % 2
                for ft in range(part * FT // 2, (part + 1) * FT // 2):
                    ins = pe.matmul(region[bank][:, k * D:(k + 1) * D], hidden_T[:, ft, k * P:(k + 1) * P],
                                    w_out[:, ft, :], start=(ft == 0), stop=(ft == FT - 1))
                if n == 3:
                    ins.then_inc(filled[bank], 1)

            last_out = {}

            walk(pe, {"to_features": to_features_noted, "qk": qk, "v": v, "maxima": maxima,
                      "max_rows": max_rows, "scores": scores, "values": values, "normalise": normalise_noted,
                      "head_features": head_features, "heads_turned": heads_turned, "attention_out": attention_out,
                      "ffn_sum": ffn_sum, "expert_in": expert_in, "expert_out": expert_out})

        @block.vector
        def _(dve):
            v = nc.vector
            maxb = (region["max0"], region["max1"])
            dve.wait_ge(silu_exp, 1)
            v.tensor_scalar(silu[:, 1, :, :], silu[:, 0, :, :], 1.0, None, ALU.add).then_inc(silu_step, 1)
            dve.wait_ge(silu_step, 1)
            v.reciprocal(silu[:, 2, :, :], silu[:, 1, :, :]).then_inc(silu_step, 1)
            dve.wait_ge(silu_step, 2)
            v.tensor_tensor(silu[:, 0, :, :], silu[:, 2, :, :], c_T[:, :, :], ALU.mult).then_inc(silu_step, 1)
            n = 0
            for i in range(4):
                for ic in range(C):
                    dve.wait_ge(pro_filled, n + 1)
                    src = maxb[n % 2][:, 0:D]
                    if i < 2:
                        d = WIDTH[0]
                        v.tensor_copy(w_qkv[0][i][:, ic, :].rearrange("p (d h) -> p h d", d=d),
                                      src.rearrange("p (h d) -> p h d", d=d)).then_inc(pro_drained, 1)
                    else:
                        dst = w_qkv[0][2] if i == 2 else w_o[0]
                        v.tensor_copy(dst[:, ic, :], src).then_inc(pro_drained, 1)
                    n += 1
            dve.wait_ge(pro_filled, n + 1)
            v.tensor_copy(b1_T[:, :], maxb[0][:, 0:E * FT]).then_inc(pro_drained, 1)
            d = WIDTH[1]
            for t in range(2):
                for ic in range(C):
                    v.tensor_copy(w_qkv[1][t][:, ic, :].rearrange("p (c d h) -> p c h d", c=C, d=d),
                                  stage_w2[t][:, ic, :].rearrange("p (c h d) -> p c h d", c=C, d=d)).then_inc(perm_done, 1)
            dve.wait_ge(pro_filled, n + 4)
            for k, src in ((0, region["scores0"][0:BATCHES, 0:D]), (1, region["scores2"][0:BATCHES, 0:D])):
                v.tensor_scalar(gate_tmp[:, k, 0, :], src, 0.0, 2.0, ALU.is_ge, ALU.mult).then_inc(gate_step, 1)
                v.tensor_scalar(gate_tmp[:, k, 1, :], src, -1.0, None, ALU.mult).then_inc(gate_step, 1)
            dve.wait_ge(gate_step, 4)
            for k, src in ((0, region["scores0"][0:BATCHES, 0:D]), (1, region["scores2"][0:BATCHES, 0:D])):
                v.tensor_tensor(gate_tmp[:, k, 1, :], src, gate_tmp[:, k, 1, :], ALU.max).then_inc(gate_step, 1)
            dve.wait_ge(gate_step, 6)
            v.tensor_scalar(gate_tmp[:, :, 1, :], gate_tmp[:, :, 1, :], GATE_MIN, None, ALU.max).then_inc(gate_step, 1)
            dve.wait_ge(gate_step, 7)
            for k, row in ((0, 0), (1, 3)):
                v.scalar_tensor_tensor(out=mod_row[:, row, :], in0=gate_tmp[:, k, 0, :], scalar=-1.0,
                                       in1=gate_tmp[:, k, 1, :], op0=ALU.add, op1=ALU.mult).then_inc(mod_rows_made, 1)
            v.tensor_scalar(mod_row[:, 1, :], region["scores1"][0:BATCHES, D:2 * D], 1.0, None, ALU.add).then_inc(mod_rows_made, 1)
            v.tensor_copy(mod_row[:, 2, :], region["scores1"][0:BATCHES, 0:D]).then_inc(mod_rows_made, 1)
            dve.wait_ge(pro_filled, n + 5)
            cols = region["side"][:, 0:2 * C * BATCHES].rearrange("p (k b) -> p k b", b=BATCHES)
            v.tensor_copy(mod_T[:, 0:C, :], cols[:, 0:C, :]).then_inc(mod_rows_made, 1)
            v.tensor_scalar(mod_T[:, C:2 * C, :], cols[:, C:2 * C, :], 1.0, None, ALU.add).then_inc(mod_rows_made, 1)
            dve.wait_ge(mod_rows_made, 6)
            dve.wait_ge(const_made, 7)

            def inverse_root(b, n):
                a, y, t = root[:, n, 0, :], rstd[:, n, :], root[:, n, 1, :]
                step = iter(range(ROOT_STEPS))

                def then(ins):
                    done = ROOT_STEPS * b + next(step) + 1
                    ins.then_inc(rstd_made[n], 1)
                    wait(dve, rstd_made[n], done)

                then(v.tensor_scalar(a, mean_var[:, n, :, 1], LN_EPS, None, ALU.add))
                then(v.tensor_scalar(t.bitcast(I32), a.bitcast(I32), 1, None, ALU.logical_shift_right))
                then(v.tensor_scalar(y.bitcast(I32), t.bitcast(I32), -1.0, float(0x5F3759DF), ALU.mult, ALU.add))
                for _ in range(NEWTON):
                    then(v.scalar_tensor_tensor(out=t, in0=y, scalar=-0.5, in1=y, op0=ALU.mult, op1=ALU.mult))
                    then(v.tensor_tensor(t, t, a, ALU.mult))
                    then(v.scalar_tensor_tensor(out=y, in0=t, scalar=1.5, in1=y, op0=ALU.add, op1=ALU.mult))

            def layernorm(b, turn, f, n):
                src = (x_in, x1, ffn_x)[n]
                dst = normed[n % 2]
                if n == 0:
                    wait(dve, x_loaded, 16 * (b + 1))
                    v.tensor_copy(mod_cur[:, :], mod_T[:, :, bass.ds(b, 1)].rearrange("p k b -> p (k b)"))\
                        .then_inc(mod_cur_made, 1)
                elif n == 1:
                    wait(dve, x1_made, 2 * (b + 1))
                else:
                    wait(dve, ffn_x_made, T * (b + 1))
                for t in range(T):
                    v.bn_stats(stats[:, n, t, :], src[:, t, :]).then_inc(stats_made[n], 1)
                for t in range(T):
                    wait_apart(dve, stats_made[n], T * b + t + 1)
                    v.bn_aggr(mean_var[:, n, t, :], stats[:, n, t, :]).then_inc(moments_made[n], 1)
                wait(dve, moments_made[n], T * (b + 1))
                inverse_root(b, n)
                for t in range(T):
                    v.tensor_scalar(dst[:, t, :], src[:, t, :], mean_var[:, n, t, 0:1], rstd[:, n, t:t + 1],
                                    ALU.subtract, ALU.mult).then_inc(normed_made[n], 1)

            def to_features(b, turn, f, n, cc):
                if n:
                    return
                (bank, _), = f
                wait(dve, filled[bank], number(f[0], turn) + 1)
                if cc == 0:
                    wait(dve, mod_cur_made, b + 1)
                v.tensor_scalar(act_T[:, cc, :], region[bank], mod_cur[:, C + cc:C + cc + 1], mod_cur[:, cc:cc + 1],
                                ALU.mult, ALU.add).then_inc(drained[bank], 1)

            def qk(b, turn, f, a, t, oc):
                (bank, _), = f
                n = 2 * t + oc
                wait(dve, top_made[a], 4 * b + n + 1)
                if n >= 2:
                    wait(dve, split_made[a], 4 * b + n - 1)
                else:
                    other, count = previous(a, b)
                    wait(dve, split_made[other], 4 * count)
                v.tensor_tensor(rest[:, n % 2, :], region[bank], parts[t][:, 0, oc, :], ALU.subtract)\
                    .then_inc(drained[bank], 1)

            def maxima(b, turn, f, a, h, qt):
                g = h // GROUP
                bank, _ = f[0]
                (wait_apart if CAUSAL[a] else wait)(dve, filled[bank], number(f[0], turn) + 1)
                dst = neg_max[:, g % 2, h % GROUP * T + qt:h % GROUP * T + qt + 1]
                if CAUSAL[a]:
                    keys = (qt + 1) * P
                    v.tensor_tensor_reduce(region[bank][:, 0:keys], region[bank][:, 0:keys], causal[:, S - keys:S],
                                           1.0, -3e38, ALU.add, ALU.max, dst).then_inc(drained[bank], 1)
                else:
                    v.tensor_reduce(dst, region[bank], AX_X, ALU.max).then_inc(drained[bank], 1)

            def max_rows(b, turn, f, a, g):
                wait(dve, filled["misc"], number(f[0], turn) + 1)
                groups = [h // GROUP for h in HEADS]
                if g >= 2:
                    wait(dve, max_split[a], 4 * groups[a] * b + 4 * (g - 1))
                else:
                    other, count = previous(a, b)
                    wait(dve, max_split[other], 4 * groups[other] * count)
                v.tensor_scalar(max_row[:, g % 2, :], misc[0:GROUP * T, 0:P], -1.0, None, ALU.mult)\
                    .then_inc(drained["misc"], 1)

            def normalise(b, turn, f, a, g):
                groups = HEADS[a] // GROUP
                d = WIDTH[a]
                wait(dve, filled["misc"], number(f[0], turn) + 1)
                turned = misc[:, :].rearrange("p (t k r) -> p t k r", t=T, k=GROUP)
                inv = inv_sum[:, :].rearrange("p (t k) -> p t k", t=T)
                v.reciprocal(inv, turned[:, :, :, d]).then_inc(sums_inverted[a], 1)
                wait(dve, sums_inverted[a], groups * b + g + 1)
                dst = heads[:, :, g * GROUP * d:(g + 1) * GROUP * d].rearrange("p t (k d) -> p t k d", d=d)
                v.tensor_tensor(dst, turned[:, :, :, 0:d], inv.unsqueeze(3).broadcast_to([P, T, GROUP, d]), ALU.mult)\
                    .then_inc(drained["misc"], 1)

            def attention_out(b, turn, f, half):
                (bank, _), = f
                wait(dve, filled[bank], number(f[0], turn) + 1)
                if half == 0:
                    wait(dve, mod_loaded, 16 * (b + 1))
                    wait(dve, residual_loaded, 16 * (b + 1))
                    wait(dve, res_made, 2 * b)
                rows = slice(2 * half, 2 * half + 2)
                v.tensor_tensor(x1[:, rows, :], region[bank].rearrange("p (t d) -> p t d", t=2),
                                mod_bc[:, 0:1, :].broadcast_to([P, 2, D]), ALU.mult).then_inc(drained[bank], 1)
                wait(dve, drained[bank], number(f[0], turn) + 1)
                v.tensor_tensor(x1[:, rows, :], x1[:, rows, :], x_again[:, rows, :], ALU.add).then_inc(x1_made, 1)

            def ffn_input(b, turn, f):
                for t in range(T):
                    wait(dve, normed_made[1], T * b + t + 1)
                    v.tensor_tensor(ffn_x[:, t, :], normed[1][:, t, :], mod_bc[:, 1, :], ALU.mult).then_inc(ffn_scaled, 1)
                for t in range(T):
                    wait(dve, ffn_scaled, T * b + t + 1)
                    v.tensor_tensor(ffn_x[:, t, :], ffn_x[:, t, :], mod_bc[:, 2, :], ALU.add).then_inc(ffn_x_made, 1)

            def bias_part(b, turn, f):
                wait(dve, gate_loaded, 48 * (b + 1))
                wait(dve, x1_made, 2 * (b + 1))
                for j in range(2):
                    v.tensor_tensor(b2_bc[:, j, :], b2_bc[:, j, :], gb_bc[:, :], ALU.mult).then_inc(bias_gated, 1)
                wait(dve, bias_gated, 2 * b + 2)
                for j in range(2):
                    v.tensor_tensor(x_res[:, 2 * j:2 * j + 2, :], x1[:, 2 * j:2 * j + 2, :],
                                    b2_bc[:, j:j + 1, :].broadcast_to([P, 2, D]), ALU.add).then_inc(res_made, 1)
                for j in range(2):
                    v.tensor_copy(b1_cur[:, j, :], b1_T[:, bass.ds(((b * 2 + j) % E) * FT, FT)]).then_inc(b1_made, 1)

            def ffn_sum(b, turn, f, mc):
                (bank, _), = f
                wait(dve, filled[bank], number(f[0], turn) + 1)
                wait(dve, x_kept, b + 1)
                v.tensor_tensor(expert_xT[:, mc, :], region[bank], ffn_xT[:, mc, :], ALU.add).then_inc(drained[bank], 1)

            last_out = {}

            def expert_out(b, turn, f, j, n):
                if n == 0:
                    last_out[0] = f[0]
                if n < 3:
                    return
                f = [last_out[0]]
                (bank, _), = f
                wait(dve, filled[bank], number(f[0], turn) + 1)
                wait(dve, y_stored[j], 16 * b + 1)
                v.tensor_tensor(y_out[:, j, :, :], region[bank].rearrange("p (t d) -> p t d", t=2),
                                gb_bc[:, :].unsqueeze(1).broadcast_to([P, 2, D]), ALU.mult).then_inc(drained[bank], 1)
                wait(dve, drained[bank], number(f[0], turn) + 1)
                wait(dve, res_made, 2 * (b + 1))
                v.tensor_tensor(y_out[:, j, :, :], y_out[:, j, :, :], x_res[:, 2 * j:2 * j + 2, :], ALU.add)\
                    .then_inc(y_made, 1)

            walk(dve, {"layernorm": layernorm, "to_features": to_features, "qk": qk, "maxima": maxima,
                       "max_rows": max_rows, "normalise": normalise, "attention_out": attention_out,
                       "ffn_input": ffn_input, "bias_part": bias_part, "ffn_sum": ffn_sum, "expert_out": expert_out})


_INS = ["L0_attn_in_features", "L0_attn_q_proj_weight", "L0_attn_k_proj_weight", "L0_attn_v_proj_weight",
        "L0_attn_o_proj_weight", "L0_ffn_ln_g", "L0_ffn_ln_b", "L0_ffn_wq", "L0_ffn_wk", "L0_ffn_wv", "L0_ffn_wo",
        "L0_ffn_w1", "L0_ffn_b1", "L0_ffn_w2", "L0_ffn_b2", "L0_c", "L0_wmod"]
_OUTS = [((8, 512, 256), "float32")]


def kernel(**inputs):
    import concourse.bacc as _bacc
    from concourse.bass_utils import run_bass_kernel_spmd as _run

    nc = _bacc.Bacc("TRN2", target_bir_lowering=False, num_devices=1)
    arrays, args = {}, []
    for name in _INS:
        a = np.ascontiguousarray(inputs[name])
        arrays[f"in_{name}_dram"] = a
        args.append(nc.dram_tensor(f"in_{name}_dram", a.shape, mybir.dt.from_np(a.dtype), kind="ExternalInput").ap())
    for i, (shape, dtype) in enumerate(_OUTS):
        dt = mybir.dt.from_np(np.dtype(dtype))
        args.append(nc.dram_tensor(f"out_{i}_dram", shape, dt, kind="ExternalOutput").ap())
    build(nc, *args)
    r = _run(nc, [arrays], core_ids=[0])
    return r.results[0]["out_0_dram"]
```

```python
from contextlib import ExitStack

import numpy as np

import concourse.bass as bass
from concourse import mybir

F32 = mybir.dt.float32
BF16 = mybir.dt.bfloat16
I32 = mybir.dt.int32
ALU = mybir.AluOpType
ACT = mybir.ActivationFunctionType
AX_X = mybir.AxisListType.X

P = 128
LN_EPS = 1e-5
GATE_MIN = 0.25
NEWTON = 3
ROOT_STEPS = 3 + 3 * NEWTON
MASKED = -1e30
LEAD = 7

HEADS = (16, 32)
WIDTH = (16, 8)
CAUSAL = (True, False)
Q_PARTS = ((0, 1, 2, 0, 1, 0), (0, 1, 2, 0, 1, 2, 0, 1, 2))
K_PARTS = ((0, 0, 0, 1, 1, 2), (0, 1, 2, 1, 2, 0, 2, 0, 1))
M_PARTS = 3
UNIT_HEADS = 8
GROUP = 4
BATCHES = 8
LOOPS = BATCHES - 2
UNITS = ((0, 1), (2, 3, 4, 5))
PRODUCT_ROWS = 96
ZEROED_UNITS = (2, 3, 4)
T_STEPS = 4
VALUES_SLOT = 3
ROWS_SLOT = 1
NORMALISE_SLOT = 2
LN_PIECES = 5 + ROOT_STEPS


def rows_of(a):
    return WIDTH[a] * len(Q_PARTS[a])


def runs(parts):
    out = []
    for g, part in enumerate(parts):
        if out and part == out[-1][1] + out[-1][2]:
            out[-1][2] += 1
        else:
            out.append([g, part, 1])
    return out



PIECES = {"qk": 2, "v": 2, "attention_out": 2, "ffn_sum": 2, "expert_in": 2, "expert_out": 8}
SLOTS = GROUP


def in_pieces(*item):
    return [(*item, part) for part in range(PIECES[item[0]])]


def attention(main, lead, beside, handed=(), hand_on=None):
    out, waiting = [], {at: [item] for at, item in handed}
    count = max(len(main), len(lead))
    early = set()
    for p in range(count):
        for k in range(SLOTS):
            if p < len(lead) and k not in early:
                out.append(("maxima", *lead[p], k))
            early.discard(k)
            if p < len(main):
                off, a, s = main[p]
                out.append(("scores", off, a, s, k))
            out += waiting.pop((p, k), [])
            for item in beside.pop(p * SLOTS + k, []):
                if item[0] == "maxima_early":
                    if p + 1 < len(lead):
                        early.add(item[1])
                        out.append(("maxima", *lead[p + 1], item[1]))
                elif item[0] == "values_early":
                    early.add("values")
                    out.append(("values", *main[p]))
                else:
                    out.append(item)
        if p < len(main) and "values" in early:
            early.discard("values")
        elif p < len(main):
            waiting.setdefault((p + 1, VALUES_SLOT), []).append(("values", *main[p]))
        if p < len(main):
            if s % T_STEPS == T_STEPS - 1:
                waiting.setdefault((p + 3, NORMALISE_SLOT), []).append(("normalise", off, a, s // T_STEPS))
        if p < len(lead) and lead[p][2] % GROUP == GROUP - 1:
            waiting.setdefault((p + 1, ROWS_SLOT), []).append(("max_rows", lead[p][0], lead[p][1], lead[p][2] // GROUP))
    for p, k in sorted(waiting):
        if hand_on is None:
            out += waiting[p, k]
        else:
            hand_on += [((p - count, k), (i[0], i[1] - 1, *i[2:])) for i in waiting[p, k]]
    for slot in sorted(beside):
        assert slot >= count * SLOTS
        out += [item for item in beside[slot] if not item[0].endswith("_early")]
    return out


def place(plan, at, items, every=1):
    for n, item in enumerate(items):
        plan.setdefault(at + n * every, []).append(item)


def place_pieces(plan, ats, items):
    for at, item in zip(ats, items, strict=True):
        place(plan, at, in_pieces(*item))


def steps_of_attention(off, a):
    return [(off, a, s) for s in range(T_STEPS * HEADS[a] // GROUP)]


def heads_of_attention(off, a):
    return [(off, a, h) for h in range(HEADS[a])]


def layernorm_items(off, n):
    return [("layernorm", off, n, piece) for piece in range(LN_PIECES)]


def place_layernorm(plan, at, off, n, together=1):
    for piece, item in enumerate(layernorm_items(off, n)):
        place(plan, at + piece // together, [item])


def features_items(off, n):
    return [("to_features", off, n, c) for c in range(2)]


def v_items(a, off):
    return [("v", off, a, half) for half in range(2)]


def qk_items(a, off):
    return [("qk", off, a, t, oc) for t in range(2) for oc in range(2)]


def out_items(off):
    return [("attention_out", off, half) for half in range(2)]


def place_experts(plan, off, at):
    place(plan, at, [("head_features", off, 1, 0), ("head_features", off, 1, 1)], 2)
    place_pieces(plan, (at + 4, at + 8), [("ffn_sum", off, 0), ("ffn_sum", off, 1)])
    place(plan, at + 10, [("keep_x", off + 1)])
    for j, start in ((0, at + 12), (1, at + 12 + 4 * SLOTS)):
        place_pieces(plan, (start + 1, start + 2), [("expert_in", off, j, n) for n in range(2)])
        plan[start + 3] += [("gelu", off, j, n) for n in range(2)]
        plan[start + 3] += [("maxima_early", 0), ("maxima_early", 1), ("values_early",), ("maxima_early", 2), ("maxima_early", 3)]
        for n in range(2, 4):
            plan[start + 3] += [*in_pieces("expert_in", off, j, n), ("gelu", off, j, n)]
        if j == 0:
            plan[start + 3].append(("load_expert_in", off, 1))
        place(plan, start + 5, in_pieces("expert_out", off, j)[:2])
        place(plan, start + 9, in_pieces("expert_out", off, j)[2:])
        if j == 0:
            plan[start + 14].append(("load_expert_out", off, 1))


def sections():
    start = [("load_x", 0), *layernorm_items(0, 0)]
    before = [("load_mod", 0), *features_items(0, 0), ("load_x", 1)]
    for item in v_items(0, 0) + qk_items(0, 0):
        before += in_pieces(*item)
    before += [("stacks", 0, 0), ("stacks", 0, 1), *layernorm_items(1, 0), *features_items(1, 0),
               ("load_residual", 0), ("load_gate", 0)]
    ahead = heads_of_attention(0, 0) + heads_of_attention(1, 0)
    before += attention([], ahead[:LEAD], {})
    beside = {}
    place_pieces(beside, (1, 5, 9, 13), qk_items(0, 1))
    place(beside, 18, [("stacks", 1, 0)])
    place(beside, 36, [("stacks", 1, 1)])
    for item in v_items(0, 1):
        beside.setdefault(67, []).extend(in_pieces(*item))
    place(beside, 76, [("head_features", 0, 0, 0), ("head_features", 0, 0, 1)])
    place_pieces(beside, (78, 80), out_items(0))
    place(beside, 82, [("load_residual", 1)])
    place_layernorm(beside, 82, 0, 1, 4)
    place(beside, 87, [("ffn_input", 0, 0), ("ffn_input", 0, 1), ("load_mod", 1)])
    place(beside, 93, features_items(0, 1))
    place_layernorm(beside, 90, 0, 2, 4)
    place(beside, 96, features_items(0, 2))
    place_pieces(beside, (98, 100), v_items(1, 0))
    place_pieces(beside, (103, 106, 109, 112), qk_items(1, 0))
    place(beside, 114, [("stacks", 0, 2), ("stacks", 0, 3), ("keep_v", 0), ("keep_x", 0)])
    first = []
    before += attention(steps_of_attention(0, 0) + steps_of_attention(1, 0), ahead[LEAD:], beside, hand_on=first)
    first = [(at, (i[0], i[1] + 1, *i[2:])) for at, i in first]
    before += attention([], heads_of_attention(0, 1)[:LEAD], {})

    n1 = SLOTS * T_STEPS * HEADS[1] // GROUP
    beside = {}
    place(beside, 0, [("load_x", 2), ("load_expert_in", 0, 0), ("load_expert_out", 0, 0), ("stacks", 0, 4)])
    place(beside, 2, [("bias_part", 0, 0), ("bias_columns", 0)])
    place(beside, 12, [("head_features", 1, 0, 0), ("head_features", 1, 0, 1)], 2)
    place_layernorm(beside, 12, 2, 0)
    place_pieces(beside, (22, 27), out_items(1))
    place(beside, 28, [("load_residual", 2)])
    place(beside, 30, features_items(2, 0), 2)
    place_pieces(beside, (34, 37), v_items(0, 2))
    place(beside, 35, [("stacks", 0, 5)])
    place_pieces(beside, (40, 44, 48, 52), qk_items(0, 2))
    place(beside, 32, layernorm_items(1, 1), 2)
    place(beside, 66, [("ffn_input", 1, 0), ("ffn_input", 1, 1), ("load_mod", 2)])
    place(beside, 78, features_items(1, 1), 2)
    place_layernorm(beside, 76, 1, 2)
    place(beside, 71, [("stacks", 2, 0)])
    place(beside, 96, features_items(1, 2), 2)
    place_pieces(beside, (100, 104), v_items(1, 1))
    place(beside, 103, [("stacks", 2, 1)])
    place_pieces(beside, (108, 112, 117, 121), qk_items(1, 1))
    place(beside, n1 + 7, [("stacks", 1, 2), ("keep_v", 1)])
    place(beside, n1 + 35, [("stacks", 1, 3)])
    place_experts(beside, 0, n1 + 12)
    place(beside, n1 + 64, [("load_gate", 1)])
    ahead = heads_of_attention(0, 1)[LEAD:] + heads_of_attention(2, 0) + heads_of_attention(1, 1)[:LEAD]
    left = []
    loop = attention(steps_of_attention(0, 1) + steps_of_attention(2, 0), ahead, beside, first, left)
    assert first == left

    beside = {}
    place(beside, 0, [("stacks", 0, 4), ("load_expert_in", 0, 0), ("load_expert_out", 0, 0)])
    place(beside, 2, [("bias_part", 0, 0), ("bias_columns", 0)])
    place(beside, 12, [("head_features", 1, 0, 0), ("head_features", 1, 0, 1)], 2)
    place_pieces(beside, (15, 18), out_items(1))
    place_layernorm(beside, 20, 1, 1, 2)
    place(beside, 29, [("ffn_input", 1, 0), ("ffn_input", 1, 1)])
    place(beside, 40, features_items(1, 1), 2)
    place_layernorm(beside, 36, 1, 2, 2)
    place(beside, 35, [("stacks", 0, 5)])
    place(beside, 50, features_items(1, 2), 2)
    place_pieces(beside, (54, 58), v_items(1, 1))
    place_pieces(beside, (63, 68, 73, 78), qk_items(1, 1))
    for u, at in zip(UNITS[1], (88, 103, 135, 167), strict=True):
        place(beside, at, [("stacks", 1, u)])
    place(beside, n1 + 3, [("keep_v", 1)])
    place_experts(beside, 0, n1 + 12)
    place(beside, n1 + 48, [("load_gate", 1), ("load_expert_in", 1, 0), ("load_expert_out", 1, 0)])
    place(beside, n1 + 56, [("bias_part", 1, 0), ("bias_columns", 1)])
    place_experts(beside, 1, 2 * n1)
    ahead = heads_of_attention(0, 1)[LEAD:] + heads_of_attention(1, 1)
    after = attention(steps_of_attention(0, 1) + steps_of_attention(1, 1), ahead, beside, first)
    after = [item for item in after if item != ("keep_x", 2)]
    return (("start", start), ("before", before), ("loop", loop), ("after", after))


def banks_of(item):
    kind = item[0]
    if kind == "scores":
        return ["scores%d" % (item[4] % 2)]
    if kind == "maxima":
        return ["max%d" % ((GROUP * item[3] + item[4]) % 3)]
    if kind in ("max_rows", "normalise", "head_features", "attention_out"):
        return ["misc"]
    if kind == "values":
        return ["out"] if item[3] % 4 == 0 else []
    if kind in ("to_features", "qk", "v", "ffn_sum", "expert_out"):
        return ["side"]
    if kind == "expert_in":
        return [("side", "misc")[item[3] % 2]]
    return []


BANKS = ("scores0", "scores1", "max0", "max1", "max2", "out", "misc", "side")


def number_fills(plan):
    begun = dict.fromkeys(BANKS, 0)
    fills, per_loop = {}, {}
    for name, items in plan:
        count = dict.fromkeys(BANKS, 0)
        unfinished = set()
        assert len(set(items)) == len(items)
        for item in items:
            if item[0] in PIECES and item[-1]:
                fills[name, item] = fills[name, (*item[:-1], 0)]
                if item[-1] == PIECES[item[0]] - 1:
                    unfinished.remove(fills[name, item][0][0])
                continue
            fills[name, item] = []
            for bank in banks_of(item):
                assert bank not in unfinished, (name, item)
                if item[0] in PIECES:
                    unfinished.add(bank)
                fills[name, item].append((bank, begun[bank] + count[bank]))
                count[bank] += 1
        turns = (LOOPS if name == "loop" else 1)
        if name == "loop":
            per_loop = count
        for bank in BANKS:
            begun[bank] += turns * count[bank]
    return fills, per_loop


def build(nc, x, wq1, wk1, wv1, wo1, ln_g, ln_b, wq2, wk2, wv2, wo2, w1, b1, w2, b2, c, wmod, out):
    _, S, D = x.shape
    E, _, F = w1.shape
    T = S // P
    C = D // P
    FT = F // P
    EXP_TOK = S // 2
    assert S == 512 and D == 256 and T == 4 and C == 2 and EXP_TOK == 256

    plan = sections()
    fills, per_loop = number_fills(plan)

    q_dram = [nc.dram_tensor("q_parts0", (2, 3, D, S), BF16, kind="Internal").ap(),
              nc.dram_tensor("q_parts1", (2, C, 3, P, S), BF16, kind="Internal").ap()]
    k_dram = [nc.dram_tensor("k_parts0", (2, 3, D, S), BF16, kind="Internal").ap(),
              nc.dram_tensor("k_parts1", (2, C, 3, P, S), BF16, kind="Internal").ap()]
    zero_dram = nc.dram_tensor("zero_rows", (PRODUCT_ROWS - rows_of(1), UNIT_HEADS * S), BF16, kind="Internal").ap()
    mod_dram = nc.dram_tensor("mod_rows", (BATCHES, 4 * D), F32, kind="Internal").ap()

    with ExitStack() as ctx:
        def sb(name, shape, dt=F32):
            return ctx.enter_context(nc.sbuf_tensor(name, shape, dt))

        def psum(name, shape):
            return ctx.enter_context(nc.psum_tensor(name, shape, F32))

        def sem(name):
            return ctx.enter_context(nc.semaphore(name))

        region = {b: psum("bank_" + b, [P, 512])[:, :] for b in BANKS}
        outb, misc = region["out"], region["misc"]

        ident = sb("ident", [P, P])
        causal = sb("causal", [P, S])
        zeros = sb("zeros", [P, P], BF16)
        q_stack = [sb("q_stack%d" % n, [P, UNIT_HEADS, S], BF16) for n in range(3)]
        k_stack = [sb("k_stack%d" % n, [P, UNIT_HEADS, S], BF16) for n in range(3)]
        probs = [sb("probs%d" % n, [P, GROUP, S]) for n in range(2)]
        v_tile = [sb("v_tile%d" % a, [P, T, HEADS[a], WIDTH[a] + 1]) for a in range(2)]
        w_qkv = [[sb("w%s%d" % (n, a), [P, C, D]) for n in "qkv"] for a in range(2)]
        w_o = [sb("wo%d" % a, [P, C, D]) for a in range(2)]
        w_in = sb("w_in", [P, C, F])
        w_out = sb("w_out", [P, FT, D])
        v_next = sb("v_next", [P, T, HEADS[1], WIDTH[1]])
        x_in = sb("x_in", [P, T, D])
        x_again = sb("x_again", [P, T, D])
        x1 = sb("x1", [P, T, D])
        x_res = sb("x_res", [P, T, D])
        normed = [sb("normed%d" % n, [P, T, D]) for n in range(2)]
        ffn_x = normed[1]
        ffn_xT_next = sb("ffn_xT_next", [P, C, S])
        ffn_xT = sb("ffn_xT", [P, C, S])
        act_T = sb("act_T", [P, C, S])
        parts = [sb("parts%s" % n, [P, 3, C, S], BF16) for n in "qk"]
        rest = sb("rest", [P, 2, S])
        neg_max = sb("neg_max", [P, 2, GROUP * T])
        max_row = sb("max_row", [GROUP * T, 2, P])
        max_rest = sb("max_rest", [GROUP * T, 2, P])
        max_parts = sb("max_parts", [GROUP * T, 2, M_PARTS, P], BF16)
        out_raw = sb("out_raw", [P, 2, S])
        inv_sum = sb("inv_sum", [P, T * GROUP])
        heads = sb("heads", [P, T, D])
        heads_T = sb("heads_T", [P, C, S])
        expert_xT = sb("expert_xT", [P, C, S])
        hidden_T = sb("hidden_T", [P, FT, EXP_TOK])
        y_out = sb("y_out", [P, 2, 2, D])
        mod_bc = sb("mod_bc", [P, 3, D])
        gb_bc = sb("gb_bc", [P, D])
        b2_bc = sb("b2_bc", [P, 2, D])
        mod_T = sb("mod_T", [P, 2 * C, BATCHES])
        mod_cur = sb("mod_cur", [P, 2 * C])
        b1_T = sb("b1_T", [P, E * FT])
        b1_cur = sb("b1_cur", [P, 2, FT])
        lng_T = sb("lng_T", [P, C])
        lnb_T = sb("lnb_T", [P, C])
        stats = sb("stats", [P, 3, T, 6])
        mean_var = sb("mean_var", [P, 3, T, 2])
        rstd = sb("rstd", [P, 3, T])
        root = sb("root", [P, 3, 2, T])
        c_T = sb("c_T", [P, C, BATCHES])
        silu = sb("silu", [P, 3, C, BATCHES])
        mod_row = hidden_T[0:BATCHES, 0:4, :]
        gate_tmp = hidden_T[0:BATCHES, 4:8, :].rearrange("b (k i) d -> b k i d", k=2)
        def stage(tile, at, shape):
            n = shape[0] * shape[1]
            flat_tile = tile[:, :, :].rearrange("p a s -> p (a s)")[:, 2 * at:2 * (at + n)].bitcast(F32)
            return flat_tile.rearrange("p (c d) -> p c d", c=shape[0])

        stage_w = [stage(q_stack[i % 3], C * D * (i // 3), (C, D)) for i in range(4)]
        stage_w2 = [stage(q_stack[i], C * D, (C, D)) for i in (1, 2)]
        stage_b1 = stage(q_stack[0], 2 * C * D, (1, P))[:, 0, :]
        stage_mod = probs[0][:, :, :].rearrange("p a s -> p (a s)")[:, 0:C * 768].rearrange("p (c n) -> p c n", c=C)
        stage_mod2 = probs[1][:, :, :].rearrange("p a s -> p (a s)")[:, 0:C * 768].rearrange("p (c n) -> p c n", c=C)

        filled = {b: sem("filled_" + b) for b in BANKS}
        drained = {b: sem("drained_" + b) for b in BANKS}
        const_made = sem("const_made")
        small_in = sem("small_in")
        weights_in = sem("weights_in")
        mod_in = sem("mod_in")
        silu_step = sem("silu_step")
        silu_exp = sem("silu_exp")
        pro_filled = sem("pro_filled")
        pro_drained = sem("pro_drained")
        gate_step = sem("gate_step")
        mod_rows_made = sem("mod_rows_made")
        mod_stored = sem("mod_stored")
        perm_done = sem("perm_done")
        ones_made = sem("ones_made")
        waits_passed = sem("waits_passed")
        x_loaded = sem("x_loaded")
        mod_loaded = sem("mod_loaded")
        gate_loaded = sem("gate_loaded")
        residual_loaded = sem("residual_loaded")
        v_kept = sem("v_kept")
        x_kept = sem("x_kept")
        mod_cur_made = sem("mod_cur_made")
        stats_made = [sem("stats_made%d" % n) for n in range(3)]
        moments_made = [sem("moments_made%d" % n) for n in range(3)]
        rstd_made = [sem("rstd_made%d" % n) for n in range(3)]
        normed_made = [sem("normed_made%d" % n) for n in range(3)]
        top_made = [sem("top_made%d" % a) for a in range(2)]
        second_made = [sem("second_made%d" % a) for a in range(2)]
        split_made = [sem("split_made%d" % a) for a in range(2)]
        parts_stored = [sem("parts_stored%d" % a) for a in range(2)]
        stack_loaded = [sem("stack_loaded%d" % u) for u in range(6)]
        max_split = [sem("max_split%d" % a) for a in range(2)]
        max_stored = [[sem("max_stored%d%d" % (a, n)) for n in range(2)] for a in range(2)]
        masked_made = sem("masked_made")
        values_done = [sem("values_done%d" % a) for a in range(2)]
        sums_inverted = [sem("sums_inverted%d" % a) for a in range(2)]
        x1_made = sem("x1_made")
        ffn_scaled = sem("ffn_scaled")
        ffn_x_made = sem("ffn_x_made")
        bias_gated = sem("bias_gated")
        res_made = sem("res_made")
        w_in_loaded = sem("w_in_loaded")
        w_out_loaded = sem("w_out_loaded")
        b1_made = sem("b1_made")
        y_made = sem("y_made")
        y_stored = [sem("y_stored%d" % j) for j in range(2)]

        def number(fill, turn):
            bank, n = fill
            return n if turn is None else turn * per_loop[bank] + n

        def wait(eng, semaphore, value):
            if isinstance(value, int) and value <= 0:
                return
            eng.wait_ge(semaphore, value)

        def wait_apart(eng, semaphore, value):
            wait(eng, semaphore, value)
            if not isinstance(value, int):
                eng.sem_inc(waits_passed, 1)

        def filled_by(name, item):
            return fills[name, item] if (name, item) in fills else fills[name, (*item, 0)]

        def walk(eng, share, in_pieces=False, notes=None, start=False):
            notes = {} if notes is None else notes
            for name, items in plan:
                if (name == "start") != start:
                    continue
                if not in_pieces:
                    items = [i[:-1] if i[0] in PIECES else i for i in items
                             if i[0] not in PIECES or i[-1] == PIECES[i[0]] - 1]
                if name == "loop":
                    noted = dict(notes)
                    with eng.Fori(0, LOOPS) as turn:
                        for item in items:
                            if item[0] in share:
                                share[item[0]](turn + item[1] if item[1] else turn, turn, filled_by(name, item), *item[2:])
                    for key, (bank, n) in notes.items():
                        assert noted.get(key, (bank, n - per_loop[bank])) == (bank, n - per_loop[bank])
                        notes[key] = (bank, n + (LOOPS - 1) * per_loop[bank])
                else:
                    for item in items:
                        if item[0] in share:
                            share[item[0]](item[1] + (LOOPS if name == "after" else 0), None, filled_by(name, item), *item[2:])

        def previous(a, b):
            if a == 0:
                return (1, b - 1) if not isinstance(b, int) or b > 1 else (0, b)
            return (0, b + 2) if not isinstance(b, int) or b + 2 <= BATCHES else (1, b)

        def buffer_of(u, b):
            if isinstance(b, int) and (b == 0 and u < 2 or b == BATCHES - 1 and u >= 2):
                return (u + 1) % 3
            return u % 3

        def buffer_free(u, b):
            per = 2 * T
            one, all_one = values_done[1], steps_of[1]
            if u < 2:
                if isinstance(b, int) and b < 2:
                    return values_done[0], per * b * u
                return one, all_one * (b - 2) + per * (u + 2)
            if isinstance(b, int) and b == BATCHES - 1:
                return one, all_one * (b - 1) + per * u if u < 5 else all_one * b + per
            if u == 2:
                return (values_done[0], 2 * per) if isinstance(b, int) and b == 0 else (one, all_one * b)
            if u == 5:
                return one, all_one * b + per
            return values_done[0], 2 * per * (b + 1) + per * (u - 2)

        def unit_of(a, h):
            return UNITS[a][h // UNIT_HEADS]

        stack_dmas = [len(runs(Q_PARTS[a])) + len(runs(K_PARTS[a])) for a in (0, 0, 1, 1, 1, 1)]
        for u in ZEROED_UNITS:
            stack_dmas[u] += 1
        steps_of = [T * h // GROUP for h in HEADS]

        block = ctx.enter_context(nc.Block())

        @block.sync
        def _(sp):
            for j in range(2):
                sp.sem_inc(y_stored[j], 1)
            sp.sem_inc(y_made, 1)
            def load_x(b, turn, f):
                wait_apart(sp, normed_made[0], T * b)
                sp.dma_start(x_in[:, :, :], x[b].rearrange("(t p) d -> p t d", p=P)).then_inc(x_loaded, 16)

            def load_residual(b, turn, f):
                wait_apart(sp, x1_made, 2 * b)
                sp.dma_start(x_again[:, :, :], x[b].rearrange("(t p) d -> p t d", p=P)).then_inc(residual_loaded, 16)

            def load_mod(b, turn, f):
                wait_apart(sp, ffn_x_made, T * b)
                sp.dma_start(mod_bc[:, :, :].rearrange("p v d -> p (v d)"),
                             mod_dram[b, 0:3 * D].partition_broadcast(P)).then_inc(mod_loaded, 16)

            def load_gate(b, turn, f):
                wait_apart(sp, y_made, 2 * b + 1)
                sp.dma_start(gb_bc[:, :], mod_dram[b, 3 * D:4 * D].partition_broadcast(P)).then_inc(gate_loaded, 16)
                for j in range(2):
                    sp.dma_start(b2_bc[:, j, :], b2[(b * 2 + j) % E].partition_broadcast(P)).then_inc(gate_loaded, 16)

            hidden_fill = {}

            def expert_in(b, turn, f, j, n):
                hidden_fill[0] = f[0]

            def load_expert_in(b, turn, f, j):
                e = (b * 2 + j) % E
                if j == 0:
                    wait_apart(sp, y_made, 2 * b + 1)
                else:
                    bank, _ = hidden_fill[0]
                    wait_apart(sp, filled[bank], number(hidden_fill[0], turn) + 1)
                sp.dma_start(w_in[:, :, :], w1[e].rearrange("(c p) n -> p c n", p=P)).then_inc(w_in_loaded, 16)

            def load_expert_out(b, turn, f, j):
                e = (b * 2 + j) % E
                wait_apart(sp, y_made, 2 * b + j + 1)
                sp.dma_start(w_out[:, :, :], w2[e].rearrange("(f p) n -> p f n", p=P)).then_inc(w_out_loaded, 16)

            def qk(b, turn, f, a, t, oc):
                n = 2 * t + oc
                wait_apart(sp, split_made[a], 4 * b + n + 1)
                dram = (q_dram, k_dram)[t][a][b % 2]
                dst = dram[:, oc * P:(oc + 1) * P, :] if a == 0 else dram[oc]
                sp.dma_start(dst.rearrange("i p s -> p i s"), parts[t][:, :, oc, :]).then_inc(parts_stored[a], 16)

            def stacks(b, turn, f, u):
                a = 0 if u in UNITS[0] else 1
                d = WIDTH[a]
                buf = buffer_of(u, b)
                wait_apart(sp, parts_stored[a], 16 * 4 * (b + 1))
                wait_apart(sp, *buffer_free(u, b))
                at = u % 2 * UNIT_HEADS * S
                for dram, stack, order in ((q_dram, q_stack, Q_PARTS[a]), (k_dram, k_stack, K_PARTS[a])):
                    src = dram[0][b % 2] if a == 0 else dram[1][b % 2, (u - 2) // 2]
                    src = src.rearrange("i (d h) s -> (i d) (h s)", d=d)[:, at:at + UNIT_HEADS * S]
                    dst = stack[buf][:, :, :].rearrange("p h s -> p (h s)")
                    for g, part, n in runs(order):
                        sp.dma_start(dst[g * d:(g + n) * d, :], src[part * d:(part + n) * d, :])\
                          .then_inc(stack_loaded[u], 16)
                if u in ZEROED_UNITS:
                    sp.dma_start(k_stack[buf][rows_of(1):PRODUCT_ROWS, :, :].rearrange("p h s -> p (h s)"), zero_dram[:, :])\
                      .then_inc(stack_loaded[u], 16)

            def max_rows(b, turn, f, a, g):
                groups = HEADS[a] // GROUP
                u = unit_of(a, g * GROUP)
                r, h = P - M_PARTS, g * GROUP % UNIT_HEADS
                wait_apart(sp, max_split[a], 4 * groups * b + 4 * g + 4)
                for m in range(M_PARTS):
                    dst = q_stack[buffer_of(u, b)][r + m:r + m + 1, h:h + GROUP, :].rearrange("p h (q t) -> p (h q) t", t=P)
                    sp.dma_start(dst, max_parts[:, g % 2, m, :]).then_inc(max_stored[a][g % 2], 16)

            def expert_out(b, turn, f, j):
                wait_apart(sp, y_made, 2 * b + j + 2)
                half = out[b].rearrange("(j t p) d -> j p t d", j=2, p=P)[j]
                sp.dma_start(half, y_out[:, j, :, :]).then_inc(y_stored[j], 16)

            walk(sp, {"load_x": load_x}, start=True)
            with nc.allow_non_contiguous_dma("a few kilobytes"):
                for cc in range(C):
                    sp.dma_start(c_T[:, cc, :], c[:, cc * P:(cc + 1) * P].rearrange("b p -> p b")).then_inc(small_in, 16)
                sp.dma_start(lng_T[:, :], ln_g.rearrange("(c p) -> p c", p=P)).then_inc(small_in, 16)
                sp.dma_start(lnb_T[:, :], ln_b.rearrange("(c p) -> p c", p=P)).then_inc(small_in, 16)
            sp.dma_start(stage_mod, wmod[:, 0:768].rearrange("(c p) n -> p c n", p=P)).then_inc(mod_in, 16)
            sp.dma_start(stage_mod2, wmod[:, 768:1536].rearrange("(c p) n -> p c n", p=P)).then_inc(mod_in, 16)
            sp.dma_start(stage_b1[0:E * FT, :], b1.rearrange("e (f p) -> (e f) p", p=P)).then_inc(weights_in, 16)
            for i, w in enumerate((wq1, wk1, wv1, wo1)):
                sp.dma_start(stage_w[i], w.rearrange("(c p) n -> p c n", p=P)).then_inc(weights_in, 16)
            for w, st in ((wq2, stage_w2[0]), (wk2, stage_w2[1]), (wv2, w_qkv[1][2][:, :, :]), (wo2, w_o[1][:, :, :])):
                sp.dma_start(st, w.rearrange("(c p) n -> p c n", p=P)).then_inc(weights_in, 16)
            sp.wait_ge(ones_made, 4)
            sp.dma_start(zero_dram[:, :], k_stack[0][0:PRODUCT_ROWS - rows_of(1), :, :].rearrange("p h s -> p (h s)"))\
              .then_inc(mod_stored, 16)
            sp.wait_ge(mod_rows_made, 6)
            sp.dma_start(mod_dram[:, :], mod_row[:, :, :].rearrange("b v d -> b (v d)")).then_inc(mod_stored, 16)
            sp.wait_ge(mod_stored, 32)
            sp.wait_ge(ones_made, 9)

            walk(sp, {"load_x": load_x, "load_residual": load_residual, "load_mod": load_mod, "load_gate": load_gate,
                      "load_expert_in": load_expert_in, "load_expert_out": load_expert_out, "qk": qk,
                      "stacks": stacks, "max_rows": max_rows, "expert_in": expert_in, "expert_out": expert_out})
            for j in range(2):
                sp.wait_ge(y_stored[j], 16 * BATCHES + 1)

        @block.gpsimd
        def _(pool):
            pool.memset(ident[:, :], 0.0).then_inc(const_made, 1)
            pool.memset(causal[:, :], 0.0).then_inc(const_made, 1)
            pool.memset(zeros[:, :], 0.0).then_inc(const_made, 1)
            for a in range(2):
                pool.memset(v_tile[a][:, :, :, WIDTH[a]:WIDTH[a] + 1], 1.0).then_inc(const_made, 1)
            pool.wait_ge(const_made, 5)
            pool.affine_select(out=ident[:, :], in_=ident[:, :], compare_op=ALU.not_equal, fill=1.0, base=0,
                               pattern=[[-1, P]], channel_multiplier=1).then_inc(const_made, 1)
            pool.affine_select(out=causal[:, S - P:S], in_=causal[:, S - P:S], compare_op=ALU.is_ge, fill=MASKED,
                               base=0, pattern=[[-1, P]], channel_multiplier=1).then_inc(const_made, 1)
            pool.memset(k_stack[0][:, :, :], 1.0).then_inc(ones_made, 1)
            for n in range(1, 3):
                pool.memset(k_stack[n][:, :, :], 1.0).then_inc(ones_made, 1)
            pool.wait_ge(ones_made, 3)
            for n in range(3):
                pool.memset(k_stack[n][0:P - M_PARTS, :, :], 0.0).then_inc(ones_made, 1)
            pool.wait_ge(pro_drained, 9)
            pool.wait_ge(perm_done, 4)
            for n in range(3):
                pool.memset(q_stack[n][:, :, :], 0.0).then_inc(ones_made, 1)

            def qk(b, turn, f, a, t, oc):
                n = 4 * b + 2 * t + oc
                buf = (2 * t + oc) % 2
                bank, _ = f[0]
                wait_apart(pool, drained[bank], number(f[0], turn) + 1)
                if t == 0 and oc == 0:
                    other, count = previous(a, b)
                    wait_apart(pool, parts_stored[other], 64 * count)
                pool.tensor_copy(parts[t][:, 1, oc, :], rest[:, buf, :]).then_inc(second_made[a], 1)
                wait(pool, second_made[a], n + 1)
                pool.tensor_tensor(parts[t][:, 2, oc, :], rest[:, buf, :], parts[t][:, 1, oc, :], ALU.subtract)\
                    .then_inc(split_made[a], 1)

            def max_rows(b, turn, f, a, g):
                groups = HEADS[a] // GROUP
                n = 4 * groups * b + 4 * g
                buf = g % 2
                wait(pool, drained["misc"], number(f[0], turn) + 1)
                per = [48 * (h // GROUP // 2) for h in HEADS]
                if g >= 2:
                    wait_apart(pool, max_stored[a][buf], per[a] * b + 48 * (g // 2))
                else:
                    other, count = previous(a, b)
                    wait_apart(pool, max_stored[other][buf], per[other] * count)
                pool.tensor_copy(max_parts[:, buf, 0, :], max_row[:, buf, :]).then_inc(max_split[a], 1)
                wait(pool, max_split[a], n + 1)
                pool.tensor_tensor(max_rest[:, buf, :], max_row[:, buf, :], max_parts[:, buf, 0, :], ALU.subtract)\
                    .then_inc(max_split[a], 1)
                wait_apart(pool, max_split[a], n + 2)
                pool.tensor_copy(max_parts[:, buf, 1, :], max_rest[:, buf, :]).then_inc(max_split[a], 1)
                wait(pool, max_split[a], n + 3)
                pool.tensor_tensor(max_parts[:, buf, 2, :], max_rest[:, buf, :], max_parts[:, buf, 1, :],
                                   ALU.subtract).then_inc(max_split[a], 1)

            def scores(b, turn, f, a, s, k):
                if not CAUSAL[a] or k < GROUP - 1:
                    return
                bank, _ = f[0]
                wait_apart(pool, drained[bank], number(f[0], turn) + 1)
                q0 = (s % T) * P
                tile = probs[s % 2][:, :, q0:q0 + P]
                pool.affine_select(out=tile, in_=tile, compare_op=ALU.is_ge, fill=0.0, base=0,
                                   pattern=[[0, GROUP], [1, P]], channel_multiplier=-1).then_inc(masked_made, 1)

            def ffn_input(b, turn, f, half):
                for t in range(2 * half, 2 * half + 2):
                    wait(pool, normed_made[1], T * b + t + 1)
                    pool.tensor_tensor(ffn_x[:, t, :], normed[1][:, t, :], mod_bc[:, 1, :], ALU.mult).then_inc(ffn_scaled, 1)
                for t in range(2 * half, 2 * half + 2):
                    wait(pool, ffn_scaled, T * b + t + 1)
                    pool.tensor_tensor(ffn_x[:, t, :], ffn_x[:, t, :], mod_bc[:, 2, :], ALU.add).then_inc(ffn_x_made, 1)

            def attention_out(b, turn, f, half):
                (bank, _), = f
                rows = slice(2 * half, 2 * half + 2)
                wait(pool, residual_loaded, 16 * (b + 1))
                wait(pool, drained[bank], number(f[0], turn) + 1)
                pool.tensor_tensor(x1[:, rows, :], x1[:, rows, :], x_again[:, rows, :], ALU.add).then_inc(x1_made, 1)

            def expert_out(b, turn, f, j):
                (bank, _), = f
                wait(pool, res_made, T * (b + 1))
                wait(pool, drained[bank], number(f[0], turn) + 1)
                pool.tensor_tensor(y_out[:, j, :, :], y_out[:, j, :, :], x_res[:, 2 * j:2 * j + 2, :], ALU.add)\
                    .then_inc(y_made, 1)

            def bias_part(b, turn, f, piece):
                wait(pool, gate_loaded, 48 * (b + 1))
                for j in range(2):
                    pool.tensor_tensor(b2_bc[:, j, :], b2_bc[:, j, :], gb_bc[:, :], ALU.mult).then_inc(bias_gated, 1)
                wait(pool, x1_made, 2 * (b + 1))
                for j in range(2):
                    wait(pool, bias_gated, 2 * b + j + 1)
                    for t in range(2 * j, 2 * j + 2):
                        pool.tensor_tensor(x_res[:, t, :], x1[:, t, :], b2_bc[:, j, :], ALU.add).then_inc(res_made, 1)

            walk(pool, {"qk": qk, "max_rows": max_rows, "scores": scores, "ffn_input": ffn_input, "bias_part": bias_part,
                        "attention_out": attention_out, "expert_out": expert_out})

        @block.scalar
        def _(act):
            act.wait_ge(small_in, 64)
            nc.scalar.activation(silu[:, 0, :, :], c_T[:, :, :], ACT.Exp, scale=-1.0).then_inc(silu_exp, 1)

            def qk(b, turn, f, a, t, oc):
                (bank, n), = f
                wait(act, filled[bank], number(f[0], turn) + 1)
                if t == 0 and oc == 0:
                    other, count = previous(a, b)
                    wait(act, parts_stored[other], 64 * count)
                nc.scalar.activation(parts[t][:, 0, oc, :], region[bank], ACT.Copy).then_inc(top_made[a], 1)

            def v(b, turn, f, a, half):
                (bank, n), = f
                wait(act, filled[bank], number(f[0], turn) + 1)
                d = WIDTH[a]
                dst = v_tile[0] if a == 0 else v_next
                nc.scalar.activation(dst[:, 2 * half:2 * half + 2, :, 0:d],
                                     region[bank].rearrange("p (t h d) -> p t h d", t=2, d=d), ACT.Copy)\
                    .then_inc(drained[bank], 1)

            def to_features(b, turn, f, n, cc):
                if n == 0:
                    return
                (bank, _), = f
                wait(act, filled[bank], number(f[0], turn) + 1)
                if n == 1:
                    nc.scalar.activation(ffn_xT_next[:, cc, :], region[bank], ACT.Copy).then_inc(drained[bank], 1)
                else:
                    nc.scalar.activation(act_T[:, cc, :], region[bank], ACT.Identity, bias=lnb_T[:, cc:cc + 1],
                                         scale=lng_T[:, cc:cc + 1]).then_inc(drained[bank], 1)

            def scores(b, turn, f, a, s, k):
                q0 = (s % T) * P if CAUSAL[a] else 0
                if k == 0:
                    if s >= 2:
                        wait(act, values_done[a], steps_of[a] * b + s - 1)
                    else:
                        other, count = previous(a, b)
                        wait(act, values_done[other], steps_of[other] * count - 1 + s)
                bank, _ = f[0]
                wait(act, filled[bank], number(f[0], turn) + 1)
                nc.scalar.activation(probs[s % 2][:, k, q0:S], region[bank][:, q0:S], ACT.Exp,
                                     scale=float(WIDTH[a]) ** -0.5).then_inc(drained[bank], 1)

            def values(b, turn, f, a, s):
                if s % T != T - 1:
                    return
                g = s // T
                steps = T * HEADS[a] // GROUP
                wait(act, values_done[a], steps * b + s + 1)
                groups = [h // GROUP for h in HEADS]
                if g >= 2:
                    wait(act, sums_inverted[a], groups[a] * b + g - 1)
                else:
                    other, count = previous(a, b)
                    wait(act, sums_inverted[other], groups[other] * count)
                nc.scalar.activation(out_raw[:, g % 2, :], outb[:, :], ACT.Copy).then_inc(drained["out"], 1)

            def head_features(b, turn, f, a, cc):
                (bank, _), = f
                wait(act, filled[bank], number(f[0], turn) + 1)
                nc.scalar.activation(heads_T[:, cc, :], region[bank], ACT.Copy).then_inc(drained[bank], 1)

            hidden_fill = {}

            def expert_in(b, turn, f, j, n):
                hidden_fill[n] = f[0]

            def gelu(b, turn, f, j, n):
                bank, _ = hidden_fill[n]
                wait(act, filled[bank], number(hidden_fill[n], turn) + 1)
                if n == 0:
                    wait(act, b1_made, 2 * (b + 1))
                    if j == 1:
                        wait(act, y_made, 2 * b + 2)
                for k in range(2):
                    ins = nc.scalar.activation(hidden_T[:, 2 * n + k, :], region[bank][:, k * 256:(k + 1) * 256],
                                               ACT.Gelu, bias=b1_cur[:, j, 2 * n + k:2 * n + k + 1])
                ins.then_inc(drained[bank], 1)

            def keep_v(b, turn, f):
                wait(act, values_done[1], steps_of[1] * b)
                nc.scalar.activation(v_tile[1][:, :, :, 0:WIDTH[1]], v_next[:, :, :, :], ACT.Copy).then_inc(v_kept, 1)

            def ffn_sum(b, turn, f, mc):
                sum_fill[0] = f[0]

            sum_fill = {}

            def keep_x(b, turn, f):
                if sum_fill:
                    bank, _ = sum_fill[0]
                    wait(act, drained[bank], number(sum_fill[0], turn) + 1)
                nc.scalar.activation(ffn_xT[:, :, :], ffn_xT_next[:, :, :], ACT.Copy).then_inc(x_kept, 1)

            walk(act, {"keep_v": keep_v, "keep_x": keep_x, "ffn_sum": ffn_sum,
                       "qk": qk, "v": v, "to_features": to_features, "scores": scores, "values": values,
                       "head_features": head_features, "expert_in": expert_in, "gelu": gelu})

        @block.tensor
        def _(pe):
            pe.wait_ge(const_made, 7)
            for k in range(4):
                pe.matmul(outb[:, k * P:(k + 1) * P], zeros[:, :], zeros[:, :], start=True, stop=True)
            maxb = (region["max0"], region["max1"])
            pe.wait_ge(weights_in, 16 * 9)
            n = 0
            for i in range(4):
                for ic in range(C):
                    if n >= 2:
                        pe.wait_ge(pro_drained, n - 1)
                    for oc in range(C):
                        ins = pe.transpose(maxb[n % 2][:, oc * P:(oc + 1) * P], stage_w[i][:, oc, ic * P:(ic + 1) * P],
                                           ident[:, :])
                    ins.then_inc(pro_filled, 1)
                    n += 1
            pe.wait_ge(pro_drained, n - 1)
            pe.transpose(maxb[0][:, 0:E * FT], stage_b1[0:E * FT, :], ident[0:E * FT, 0:E * FT]).then_inc(pro_filled, 1)
            pe.wait_ge(mod_in, 32)
            pe.wait_ge(silu_step, 3)
            stages = (stage_mod, stage_mod2)
            for bank, lo, hi in ((region["scores0"], 512, 768), (region["scores1"], 768, 1280), (region["max2"], 1280, 1536)):
                st, o = (stages[0], 0) if hi <= 768 else (stages[1], 768)
                for cc in range(C):
                    ins = pe.matmul(bank[0:BATCHES, 0:hi - lo], silu[:, 0, cc, :], st[:, cc, lo - o:hi - o],
                                    start=(cc == 0), stop=(cc == C - 1))
                ins.then_inc(pro_filled, 1)
            for k in range(2 * C):
                for cc in range(C):
                    ins = pe.matmul(region["side"][:, k * BATCHES:(k + 1) * BATCHES], stages[0][:, cc, k * P:(k + 1) * P],
                                    silu[:, 0, cc, :], start=(cc == 0), stop=(cc == C - 1))
            ins.then_inc(pro_filled, 1)
            pe.wait_ge(pro_drained, 9)
            pe.wait_ge(mod_rows_made, 6)
            pe.wait_ge(perm_done, 4)

            def start_fill(f, turn):
                bank, _ = f
                wait(pe, drained[bank], number(f, turn))

            def to_features(b, turn, f, n, cc):
                (bank, _), = f
                start_fill(f[0], turn)
                if n == 1:
                    wait(pe, ffn_x_made, T * (b + 1))
                    src = ffn_x
                else:
                    wait(pe, normed_made[n], T * (b + 1))
                    src = normed[n % 2]
                for t in range(T):
                    ins = pe.transpose(region[bank][:, t * P:(t + 1) * P], src[:, t, cc * P:(cc + 1) * P], ident[:, :])
                ins.then_inc(filled[bank], 1)

            def wait_drained(fs, turn, into=None):
                for bank, n in {bank: (bank, n) for bank, n in sorted(fs)}.values():
                    if bank != into:
                        wait(pe, drained[bank], number((bank, n), turn) + 1)

            features_fill, scores_fill = {}, {}

            def to_features_noted(b, turn, f, n, cc):
                to_features(b, turn, f, n, cc)
                features_fill[n, cc] = f[0]


            def qk(b, turn, f, a, t, oc, cc):
                (bank, _), = f
                if cc == 0:
                    if t == 0 and oc == 0:
                        wait_drained([features_fill[2 * a, c2] for c2 in range(C)], turn, bank)
                    start_fill(f[0], turn)
                ins = pe.matmul(region[bank], w_qkv[a][t][:, cc, oc * P:(oc + 1) * P], act_T[:, cc, :],
                                start=(cc == 0), stop=(cc == C - 1))
                if cc == C - 1:
                    ins.then_inc(filled[bank], 1)

            def v(b, turn, f, a, half, k):
                (bank, _), = f
                if k == 0:
                    if half == 0:
                        wait_drained([features_fill[2 * a, cc] for cc in range(C)], turn, bank)
                    start_fill(f[0], turn)
                t = 2 * half + k
                for cc in range(C):
                    ins = pe.matmul(region[bank][:, k * D:(k + 1) * D], act_T[:, cc, t * P:(t + 1) * P],
                                    w_qkv[a][2][:, cc, :], start=(cc == 0), stop=(cc == C - 1))
                if k == 1:
                    ins.then_inc(filled[bank], 1)

            maxima_fill = {}

            def maxima(b, turn, f, a, h, qt):
                u = unit_of(a, h)
                buf, hh, r = buffer_of(u, b), h % UNIT_HEADS, P - M_PARTS
                if hh == 0 and qt == 0:
                    wait(pe, stack_loaded[u], 16 * stack_dmas[u] * (b + 1))
                bank, _ = f[0]
                keys = (qt + 1) * P if CAUSAL[a] else S
                start_fill(f[0], turn)
                pe.matmul(region[bank][:, 0:keys], q_stack[buf][0:r, hh, qt * P:(qt + 1) * P],
                          k_stack[buf][0:r, hh, 0:keys], start=True, stop=True).then_inc(filled[bank], 1)
                maxima_fill[h // GROUP] = f[0]

            def max_rows(b, turn, f, a, g):
                bank, _ = maxima_fill[g]
                wait(pe, drained[bank], number(maxima_fill[g], turn) + 1)
                start_fill(f[0], turn)
                pe.transpose(misc[0:GROUP * T, 0:P], neg_max[:, g % 2, :], ident[:, :]).then_inc(filled["misc"], 1)

            def scores(b, turn, f, a, s, k):
                g, kt = s // T, s % T
                u = unit_of(a, g * GROUP)
                buf = buffer_of(u, b)
                q0 = kt * P if CAUSAL[a] else 0
                if kt == 0 and k == 0:
                    groups = HEADS[a] // GROUP
                    wait(pe, max_stored[a][g % 2], 48 * (groups // 2) * b + 48 * (g // 2 + 1))
                bank, _ = f[0]
                start_fill(f[0], turn)
                h = (g * GROUP + k) % UNIT_HEADS
                pe.matmul(region[bank][:, q0:S], k_stack[buf][:, h, kt * P:(kt + 1) * P], q_stack[buf][:, h, q0:S],
                          start=True, stop=True).then_inc(filled[bank], 1)
                scores_fill[s % 2] = f[0]

            def values(b, turn, f, a, s):
                g, kt = s // T, s % T
                q0 = kt * P if CAUSAL[a] else 0
                if kt == 0:
                    start_fill(f[0], turn)
                    if a == 1 and s == 0:
                        wait(pe, v_kept, b + 1)
                bank, _ = scores_fill[s % 2]
                wait(pe, drained[bank], number(scores_fill[s % 2], turn) + 1)
                if CAUSAL[a]:
                    wait(pe, masked_made, T * HEADS[a] // GROUP * b + s + 1)
                for k in range(GROUP):
                    ins = pe.matmul(outb[32 * k:32 * k + WIDTH[a] + 1, q0:S], v_tile[a][:, kt, g * GROUP + k, :],
                                    probs[s % 2][:, k, q0:S], start=(kt == 0), stop=(kt == T - 1),
                                    skip_group_check=True)
                ins.then_inc(values_done[a], 1)

            def normalise(b, turn, f, a, g):
                wait(pe, drained["out"], out_number(b, a, g) + 1)
                start_fill(f[0], turn)
                for t in range(T):
                    ins = pe.transpose(misc[:, t * P:(t + 1) * P], out_raw[:, g % 2, t * P:(t + 1) * P], ident[:, :])
                ins.then_inc(filled["misc"], 1)

            def out_number(b, a, g):
                first, second = (h // GROUP for h in HEADS)
                other, count = previous(a, b)
                if a == 0:
                    return first * b + (second * count if other == 1 else 0) + g
                return second * b + first * (count if other == 0 else BATCHES) + g

            def head_features(b, turn, f, a, cc):
                (bank, _), = f
                start_fill(f[0], turn)
                if cc == 0:
                    wait(pe, drained["misc"], number(turned_fill[0], turn) + 1)
                for t in range(T):
                    ins = pe.transpose(region[bank][:, t * P:(t + 1) * P], heads[:, t, cc * P:(cc + 1) * P], ident[:, :])
                ins.then_inc(filled[bank], 1)
                heads_fill[cc] = f[0]

            heads_fill = {}
            turned_fill = {}

            def normalise_noted(b, turn, f, a, g):
                normalise(b, turn, f, a, g)
                turned_fill[0] = f[0]

            def attention_out(b, turn, f, half, k):
                (bank, _), = f
                if k == 0:
                    start_fill(f[0], turn)
                t = 2 * half + k
                for cc in range(C):
                    ins = pe.matmul(region[bank][:, k * D:(k + 1) * D], heads_T[:, cc, t * P:(t + 1) * P],
                                    w_o[0][:, cc, :], start=(cc == 0), stop=(cc == C - 1))
                if k == 1:
                    ins.then_inc(filled[bank], 1)

            def ffn_sum(b, turn, f, mc, cc):
                (bank, _), = f
                if cc == 0:
                    wait_drained(heads_fill.values(), turn, bank)
                    start_fill(f[0], turn)
                ins = pe.matmul(region[bank], w_o[1][:, cc, mc * P:(mc + 1) * P], heads_T[:, cc, :],
                                start=(cc == 0), stop=(cc == C - 1))
                if cc == C - 1:
                    ins.then_inc(filled[bank], 1)
                sum_fill[mc] = f[0]

            sum_fill = {}
            hidden_fill = {}

            def expert_in(b, turn, f, j, n, k):
                (bank, _), = f
                if n == 0 and k == 0:
                    wait(pe, w_in_loaded, 16 * (2 * b + j + 1))
                    if j == 0:
                        wait_drained(sum_fill.values(), turn, bank)
                if k == 0:
                    start_fill(f[0], turn)
                ft = 2 * n + k
                for cc in range(C):
                    ins = pe.matmul(region[bank][:, k * EXP_TOK:(k + 1) * EXP_TOK], w_in[:, cc, ft * P:(ft + 1) * P],
                                    expert_xT[:, cc, j * EXP_TOK:(j + 1) * EXP_TOK],
                                    start=(cc == 0), stop=(cc == C - 1))
                if k == 1:
                    ins.then_inc(filled[bank], 1)
                hidden_fill[n] = f[0]

            def expert_out(b, turn, f, j, part):
                (bank, _), = f
                if part == 0:
                    wait(pe, w_out_loaded, 16 * (2 * b + j + 1))
                    wait_drained(hidden_fill.values(), turn, bank)
                    start_fill(f[0], turn)
                k, first = part // 4, part % 4 * 2
                for ft in range(first, first + 2):
                    ins = pe.matmul(region[bank][:, k * D:(k + 1) * D], hidden_T[:, ft, k * P:(k + 1) * P],
                                    w_out[:, ft, :], start=(ft == 0), stop=(ft == FT - 1))
                if part == 7:
                    ins.then_inc(filled[bank], 1)

            walk(pe, {"to_features": to_features_noted, "qk": qk, "v": v, "maxima": maxima,
                      "max_rows": max_rows, "scores": scores, "values": values, "normalise": normalise_noted,
                      "head_features": head_features, "attention_out": attention_out, "ffn_sum": ffn_sum,
                      "expert_in": expert_in, "expert_out": expert_out}, in_pieces=True, notes=scores_fill)

        @block.vector
        def _(dve):
            v = nc.vector
            maxb = (region["max0"], region["max1"])
            def inverse_root(b, n, part):
                a, y, t = root[:, n, 0, :], rstd[:, n, :], root[:, n, 1, :]

                def then(ins):
                    ins.then_inc(rstd_made[n], 1)

                if part:
                    wait(dve, rstd_made[n], ROOT_STEPS * b + part)

                if part == 0:
                    then(v.tensor_scalar(a, mean_var[:, n, :, 1], LN_EPS, None, ALU.add))
                elif part == 1:
                    then(v.tensor_scalar(t.bitcast(I32), a.bitcast(I32), 1, None, ALU.logical_shift_right))
                elif part == 2:
                    then(v.tensor_scalar(y.bitcast(I32), t.bitcast(I32), -1.0, float(0x5F3759DF), ALU.mult, ALU.add))
                elif part % 3 == 0:
                    then(v.scalar_tensor_tensor(out=t, in0=y, scalar=-0.5, in1=y, op0=ALU.mult, op1=ALU.mult))
                elif part % 3 == 1:
                    then(v.tensor_tensor(t, t, a, ALU.mult))
                else:
                    then(v.scalar_tensor_tensor(out=y, in0=t, scalar=1.5, in1=y, op0=ALU.add, op1=ALU.mult))

            def layernorm(b, turn, f, n, piece):
                src = (x_in, x1, ffn_x)[n]
                dst = normed[n % 2]
                if n == 0 and piece == 0:
                    wait(dve, x_loaded, 16 * (b + 1))
                elif n == 1 and piece < 2:
                    wait(dve, x1_made, 2 * b + piece + 1)
                elif n == 2 and piece < 2:
                    wait(dve, ffn_x_made, T * b + 2 * piece + 2)
                if piece < 2:
                    for t in range(2 * piece, 2 * piece + 2):
                        v.bn_stats(stats[:, n, t, :], src[:, t, :]).then_inc(stats_made[n], 1)
                elif piece == 2:
                    for t in range(T):
                        wait_apart(dve, stats_made[n], T * b + t + 1)
                        v.bn_aggr(mean_var[:, n, t, :], stats[:, n, t, :]).then_inc(moments_made[n], 1)
                elif piece < 3 + ROOT_STEPS:
                    if piece == 3:
                        wait(dve, moments_made[n], T * (b + 1))
                    inverse_root(b, n, piece - 3)
                else:
                    half = piece - 3 - ROOT_STEPS
                    if half == 0:
                        wait(dve, rstd_made[n], ROOT_STEPS * (b + 1))
                    for t in range(2 * half, 2 * half + 2):
                        v.tensor_scalar(dst[:, t, :], src[:, t, :], mean_var[:, n, t, 0:1], rstd[:, n, t:t + 1],
                                        ALU.subtract, ALU.mult).then_inc(normed_made[n], 1)

            def to_features(b, turn, f, n, cc):
                if n:
                    return
                (bank, _), = f
                if cc == 0:
                    v.tensor_copy(mod_cur[:, :], mod_T[:, :, bass.ds(b, 1)].rearrange("p k b -> p (k b)"))\
                        .then_inc(mod_cur_made, 1)
                wait(dve, filled[bank], number(f[0], turn) + 1)
                if cc == 0:
                    wait(dve, mod_cur_made, b + 1)
                v.tensor_scalar(act_T[:, cc, :], region[bank], mod_cur[:, C + cc:C + cc + 1], mod_cur[:, cc:cc + 1],
                                ALU.mult, ALU.add).then_inc(drained[bank], 1)

            def qk(b, turn, f, a, t, oc):
                (bank, _), = f
                n = 2 * t + oc
                wait(dve, top_made[a], 4 * b + n + 1)
                if n >= 2:
                    wait(dve, split_made[a], 4 * b + n - 1)
                else:
                    other, count = previous(a, b)
                    wait(dve, split_made[other], 4 * count)
                v.tensor_tensor(rest[:, n % 2, :], region[bank], parts[t][:, 0, oc, :], ALU.subtract)\
                    .then_inc(drained[bank], 1)

            def maxima(b, turn, f, a, h, qt):
                g = h // GROUP
                bank, _ = f[0]
                (wait_apart if CAUSAL[a] else wait)(dve, filled[bank], number(f[0], turn) + 1)
                dst = neg_max[:, g % 2, h % GROUP * T + qt:h % GROUP * T + qt + 1]
                if CAUSAL[a]:
                    keys = (qt + 1) * P
                    v.tensor_tensor_reduce(region[bank][:, 0:keys], region[bank][:, 0:keys], causal[:, S - keys:S],
                                           1.0, -3e38, ALU.add, ALU.max, dst).then_inc(drained[bank], 1)
                else:
                    v.tensor_reduce(dst, region[bank], AX_X, ALU.max).then_inc(drained[bank], 1)

            def max_rows(b, turn, f, a, g):
                wait(dve, filled["misc"], number(f[0], turn) + 1)
                groups = [h // GROUP for h in HEADS]
                if g >= 2:
                    wait(dve, max_split[a], 4 * groups[a] * b + 4 * (g - 1))
                else:
                    other, count = previous(a, b)
                    wait(dve, max_split[other], 4 * groups[other] * count)
                v.tensor_scalar(max_row[:, g % 2, :], misc[0:GROUP * T, 0:P], -1.0, None, ALU.mult)\
                    .then_inc(drained["misc"], 1)

            def normalise(b, turn, f, a, g):
                groups = HEADS[a] // GROUP
                d = WIDTH[a]
                wait(dve, filled["misc"], number(f[0], turn) + 1)
                turned = misc[:, :].rearrange("p (t k r) -> p t k r", t=T, k=GROUP)
                inv = inv_sum[:, :].rearrange("p (t k) -> p t k", t=T)
                v.reciprocal(inv, turned[:, :, :, d]).then_inc(sums_inverted[a], 1)
                wait(dve, sums_inverted[a], groups * b + g + 1)
                dst = heads[:, :, g * GROUP * d:(g + 1) * GROUP * d].rearrange("p t (k d) -> p t k d", d=d)
                v.tensor_tensor(dst, turned[:, :, :, 0:d], inv.unsqueeze(3).broadcast_to([P, T, GROUP, d]), ALU.mult)\
                    .then_inc(drained["misc"], 1)

            def attention_out(b, turn, f, half):
                (bank, _), = f
                wait(dve, filled[bank], number(f[0], turn) + 1)
                if half == 0:
                    wait(dve, mod_loaded, 16 * (b + 1))
                    wait(dve, res_made, T * b)
                rows = slice(2 * half, 2 * half + 2)
                v.tensor_tensor(x1[:, rows, :], region[bank].rearrange("p (t d) -> p t d", t=2),
                                mod_bc[:, 0:1, :].broadcast_to([P, 2, D]), ALU.mult).then_inc(drained[bank], 1)

            def bias_columns(b, turn, f):
                if not isinstance(b, int) or b > 0:
                    wait(dve, y_made, 2 * b + 1)
                for j in range(2):
                    v.tensor_copy(b1_cur[:, j, :], b1_T[:, bass.ds(((b * 2 + j) % E) * FT, FT)]).then_inc(b1_made, 1)

            def ffn_sum(b, turn, f, mc):
                (bank, _), = f
                wait(dve, filled[bank], number(f[0], turn) + 1)
                wait(dve, x_kept, b + 1)
                v.tensor_tensor(expert_xT[:, mc, :], region[bank], ffn_xT[:, mc, :], ALU.add).then_inc(drained[bank], 1)

            def expert_out(b, turn, f, j):
                (bank, _), = f
                wait(dve, filled[bank], number(f[0], turn) + 1)
                wait(dve, y_stored[j], 16 * b + 1)
                v.tensor_tensor(y_out[:, j, :, :], region[bank].rearrange("p (t d) -> p t d", t=2),
                                gb_bc[:, :].unsqueeze(1).broadcast_to([P, 2, D]), ALU.mult).then_inc(drained[bank], 1)

            walk(dve, {"layernorm": layernorm}, start=True)
            dve.wait_ge(silu_exp, 1)
            v.tensor_scalar(silu[:, 1, :, :], silu[:, 0, :, :], 1.0, None, ALU.add).then_inc(silu_step, 1)
            dve.wait_ge(silu_step, 1)
            v.reciprocal(silu[:, 2, :, :], silu[:, 1, :, :]).then_inc(silu_step, 1)
            dve.wait_ge(silu_step, 2)
            v.tensor_tensor(silu[:, 0, :, :], silu[:, 2, :, :], c_T[:, :, :], ALU.mult).then_inc(silu_step, 1)
            n = 0
            for i in range(4):
                for ic in range(C):
                    dve.wait_ge(pro_filled, n + 1)
                    src = maxb[n % 2][:, 0:D]
                    if i < 2:
                        d = WIDTH[0]
                        v.tensor_copy(w_qkv[0][i][:, ic, :].rearrange("p (d h) -> p h d", d=d),
                                      src.rearrange("p (h d) -> p h d", d=d)).then_inc(pro_drained, 1)
                    else:
                        dst = w_qkv[0][2] if i == 2 else w_o[0]
                        v.tensor_copy(dst[:, ic, :], src).then_inc(pro_drained, 1)
                    n += 1
            dve.wait_ge(pro_filled, n + 1)
            v.tensor_copy(b1_T[:, :], maxb[0][:, 0:E * FT]).then_inc(pro_drained, 1)
            d = WIDTH[1]
            for t in range(2):
                for ic in range(C):
                    v.tensor_copy(w_qkv[1][t][:, ic, :].rearrange("p (c d h) -> p c h d", c=C, d=d),
                                  stage_w2[t][:, ic, :].rearrange("p (c h d) -> p c h d", c=C, d=d)).then_inc(perm_done, 1)
            dve.wait_ge(pro_filled, n + 4)
            for k, src in ((0, region["scores0"][0:BATCHES, 0:D]), (1, region["max2"][0:BATCHES, 0:D])):
                v.tensor_scalar(gate_tmp[:, k, 0, :], src, 0.0, 2.0, ALU.is_ge, ALU.mult).then_inc(gate_step, 1)
                v.tensor_scalar(gate_tmp[:, k, 1, :], src, -1.0, None, ALU.mult).then_inc(gate_step, 1)
            dve.wait_ge(gate_step, 4)
            for k, src in ((0, region["scores0"][0:BATCHES, 0:D]), (1, region["max2"][0:BATCHES, 0:D])):
                v.tensor_tensor(gate_tmp[:, k, 1, :], src, gate_tmp[:, k, 1, :], ALU.max).then_inc(gate_step, 1)
            dve.wait_ge(gate_step, 6)
            v.tensor_scalar(gate_tmp[:, :, 1, :], gate_tmp[:, :, 1, :], GATE_MIN, None, ALU.max).then_inc(gate_step, 1)
            dve.wait_ge(gate_step, 7)
            for k, row in ((0, 0), (1, 3)):
                v.scalar_tensor_tensor(out=mod_row[:, row, :], in0=gate_tmp[:, k, 0, :], scalar=-1.0,
                                       in1=gate_tmp[:, k, 1, :], op0=ALU.add, op1=ALU.mult).then_inc(mod_rows_made, 1)
            v.tensor_scalar(mod_row[:, 1, :], region["scores1"][0:BATCHES, D:2 * D], 1.0, None, ALU.add).then_inc(mod_rows_made, 1)
            v.tensor_copy(mod_row[:, 2, :], region["scores1"][0:BATCHES, 0:D]).then_inc(mod_rows_made, 1)
            dve.wait_ge(pro_filled, n + 5)
            cols = region["side"][:, 0:2 * C * BATCHES].rearrange("p (k b) -> p k b", b=BATCHES)
            v.tensor_copy(mod_T[:, 0:C, :], cols[:, 0:C, :]).then_inc(mod_rows_made, 1)
            v.tensor_scalar(mod_T[:, C:2 * C, :], cols[:, C:2 * C, :], 1.0, None, ALU.add).then_inc(mod_rows_made, 1)
            dve.wait_ge(mod_rows_made, 6)
            dve.wait_ge(const_made, 7)

            walk(dve, {"layernorm": layernorm, "to_features": to_features, "qk": qk, "maxima": maxima,
                       "max_rows": max_rows, "normalise": normalise, "attention_out": attention_out,
                       "bias_columns": bias_columns, "ffn_sum": ffn_sum, "expert_out": expert_out})


_INS = ["L0_attn_in_features", "L0_attn_q_proj_weight", "L0_attn_k_proj_weight", "L0_attn_v_proj_weight",
        "L0_attn_o_proj_weight", "L0_ffn_ln_g", "L0_ffn_ln_b", "L0_ffn_wq", "L0_ffn_wk", "L0_ffn_wv", "L0_ffn_wo",
        "L0_ffn_w1", "L0_ffn_b1", "L0_ffn_w2", "L0_ffn_b2", "L0_c", "L0_wmod"]
_OUTS = [((8, 512, 256), "float32")]


def kernel(**inputs):
    import concourse.bacc as _bacc
    from concourse.bass_utils import run_bass_kernel_spmd as _run

    nc = _bacc.Bacc("TRN2", target_bir_lowering=False, num_devices=1)
    arrays, args = {}, []
    for name in _INS:
        a = np.ascontiguousarray(inputs[name])
        arrays[f"in_{name}_dram"] = a
        args.append(nc.dram_tensor(f"in_{name}_dram", a.shape, mybir.dt.from_np(a.dtype), kind="ExternalInput").ap())
    for i, (shape, dtype) in enumerate(_OUTS):
        dt = mybir.dt.from_np(np.dtype(dtype))
        args.append(nc.dram_tensor(f"out_{i}_dram", shape, dt, kind="ExternalOutput").ap())
    build(nc, *args)
    r = _run(nc, [arrays], core_ids=[0])
    return r.results[0]["out_0_dram"]
```
